# Optimizing a Trainium2 kernel written in Bass

```python
import numpy as np
import jax
import jax.numpy as jnp

def _softmax(x, axis=-1):
    return jax.nn.softmax(x, axis=axis)

def _gelu(x):
    return jax.nn.gelu(x, approximate=True)

def _silu(x):
    return jax.nn.silu(x)

def _sigmoid(x):
    return jax.nn.sigmoid(x)

def _layernorm(x, axis=-1, eps=1e-05):
    m = jnp.mean(x, axis=axis, keepdims=True)
    v = jnp.var(x, axis=axis, keepdims=True)
    return (x - m) / jnp.sqrt(v + eps)

def _scatter_add(tgt, idx, src, axis=0):
    return tgt.at[idx].add(src)

def _segment_sum(src, seg, n):
    return jax.ops.segment_sum(src, seg, n)
kernel_name = 'mk_xattn_ffn_d1_seqx_r4_db2129'

def setup_inputs(seed: int=0):
    np.random.seed(seed)
    _w = jnp.asarray

    def _rec_inputs():
        import jax
        import jax.numpy as jnp
        _rk = jax.random.key(seed)
        x = -0.0005207 + 1.001 * jax.random.normal(jax.random.fold_in(_rk, 1), (16, 256, 256), jnp.float32)
        _lenS = 256 - jax.random.randint(jax.random.fold_in(_rk, 7), (16,), 0, max(1, 256 // 4) + 1, jnp.int32)
        _lenS2 = 77 - jax.random.randint(jax.random.fold_in(_rk, 8), (16,), 0, max(1, 77 // 4) + 1, jnp.int32)
        _ctx_1024P = jax.random.normal(jax.random.fold_in(_rk, 11), (16, 16, 256), jnp.float32)
        _ctx_1024c = jax.random.dirichlet(jax.random.fold_in(_rk, 511), 0.3 * jnp.ones((16,), jnp.float32), (16, 77))
        _ctx_1024t = jnp.einsum('bsk,bkd->bsd', _ctx_1024c, _ctx_1024P)
        _ctx_1024t = _ctx_1024t * jax.lax.rsqrt(jnp.mean(jnp.square(_ctx_1024t)) + 1e-12) * 0.953939
        ctx_1024 = 4.13588e-05 + 0.999923 * (_ctx_1024t + 0.3 * jax.random.normal(jax.random.fold_in(_rk, 611), (16, 77, 256), jnp.float32))
        return (x, ctx_1024)
    x, ctx_1024 = _rec_inputs()

    def _L0_xattn_setup():
        import jax, jax.numpy as jnp
        import numpy as np
        WIDTH = 256
        DATA_WIDTH = 256
        HEADS = 16
        INIT_SCALE = 0.02
        key = jax.random.key(seed)
        ks = jax.random.split(key, 8)
        x = jax.random.normal(ks[0], (2, 256, WIDTH), dtype=jnp.float32)
        data = jax.random.normal(ks[1], (2, 1024, DATA_WIDTH), dtype=jnp.float32)
        Wq = jax.random.normal(ks[2], (WIDTH, WIDTH), dtype=jnp.float32) * INIT_SCALE
        bq = jnp.zeros((WIDTH,), dtype=jnp.float32)
        Wkv = jax.random.normal(ks[3], (DATA_WIDTH, 2 * WIDTH), dtype=jnp.float32) * INIT_SCALE
        bkv = jnp.zeros((2 * WIDTH,), dtype=jnp.float32)
        Wp = jax.random.normal(ks[4], (WIDTH, WIDTH), dtype=jnp.float32) * INIT_SCALE
        bp = jnp.zeros((WIDTH,), dtype=jnp.float32)
        return {'x': x, 'data': data, 'Wq': Wq, 'bq': bq, 'Wkv': Wkv, 'bkv': bkv, 'Wp': Wp, 'bp': bp}
    _L0_xattn_all = _L0_xattn_setup()
    _L0_xattn_in = {k: v for k, v in _L0_xattn_all.items() if k in ('Wq', 'bq', 'Wkv', 'bkv', 'Wp', 'bp')}
    del _L0_xattn_all

    def _L0_ffn_setup():
        import jax, jax.numpy as jnp
        import numpy as np
        D, H, E, K = (256, 1024, 8, 2)
        B, T = (2, 512)

        def _layernorm(x, g, b, eps=1e-05):
            mu = jnp.mean(x, axis=-1, keepdims=True)
            var = jnp.mean(jnp.square(x - mu), axis=-1, keepdims=True)
            return (x - mu) * jax.lax.rsqrt(var + eps) * g + b

        def _expert(x, g, b, W1, b1, W2, b2, Wo, bo):
            x = _layernorm(x, g, b)
            x1 = x @ W1 + b1
            x2 = jnp.clip(x @ W2 + b2, -20.0, 20.0)
            hidden = jnp.clip(x1 * (x2 * jax.nn.sigmoid(x2)), -10000.0, 10000.0)
            return jnp.clip(hidden @ Wo + bo, -10000.0, 10000.0)
        key = jax.random.key(seed)
        ks = jax.random.split(key, 6)
        s = 0.02
        return {'x': jax.random.normal(ks[0], (B, T, D), jnp.float32), 'ln_g': jnp.ones((D,), jnp.float32), 'ln_b': jnp.zeros((D,), jnp.float32), 'router_w': jax.random.normal(ks[1], (D, E), jnp.float32) * s, 'eg': jnp.ones((E, D), jnp.float32), 'eb': jnp.zeros((E, D), jnp.float32), 'W1': jax.random.normal(ks[2], (E, D, H), jnp.float32) * s, 'b1': jnp.zeros((E, H), jnp.float32), 'W2': jax.random.normal(ks[3], (E, D, H), jnp.float32) * s, 'b2': jnp.zeros((E, H), jnp.float32), 'Wo': jax.random.normal(ks[4], (E, H, D), jnp.float32) * s, 'bo': jnp.zeros((E, D), jnp.float32)}
    _L0_ffn_all = _L0_ffn_setup()
    _L0_ffn_in = {k: v for k, v in _L0_ffn_all.items() if k in ('ln_g', 'ln_b', 'router_w', 'eg', 'eb', 'W1', 'b1', 'W2', 'b2', 'Wo', 'bo')}
    del _L0_ffn_all
    return {'x': x, 'ctx_1024': ctx_1024, 'L0_xattn_Wq': _L0_xattn_in['Wq'], 'L0_xattn_bq': _L0_xattn_in['bq'], 'L0_xattn_Wkv': _L0_xattn_in['Wkv'], 'L0_xattn_bkv': _L0_xattn_in['bkv'], 'L0_xattn_Wp': _L0_xattn_in['Wp'], 'L0_xattn_bp': _L0_xattn_in['bp'], 'L0_ffn_ln_g': _L0_ffn_in['ln_g'], 'L0_ffn_ln_b': _L0_ffn_in['ln_b'], 'L0_ffn_router_w': _L0_ffn_in['router_w'], 'L0_ffn_eg': _L0_ffn_in['eg'], 'L0_ffn_eb': _L0_ffn_in['eb'], 'L0_ffn_W1': _L0_ffn_in['W1'], 'L0_ffn_b1': _L0_ffn_in['b1'], 'L0_ffn_W2': _L0_ffn_in['W2'], 'L0_ffn_b2': _L0_ffn_in['b2'], 'L0_ffn_Wo': _L0_ffn_in['Wo'], 'L0_ffn_bo': _L0_ffn_in['bo']}

def reference(x, ctx_1024, L0_xattn_Wq, L0_xattn_bq, L0_xattn_Wkv, L0_xattn_bkv, L0_xattn_Wp, L0_xattn_bp, L0_ffn_ln_g, L0_ffn_ln_b, L0_ffn_router_w, L0_ffn_eg, L0_ffn_eb, L0_ffn_W1, L0_ffn_b1, L0_ffn_W2, L0_ffn_b2, L0_ffn_Wo, L0_ffn_bo):
    import jax
    import jax.numpy as jnp

    def _L0_xattn_ref(x, data, Wq, bq, Wkv, bkv, Wp, bp):
        import jax, jax.numpy as jnp
        import numpy as np
        WIDTH = 256
        DATA_WIDTH = 256
        HEADS = 16
        INIT_SCALE = 0.02
        bs, n_ctx, _ = x.shape
        _, n_data, _ = data.shape
        d = WIDTH // HEADS
        q = (x @ Wq + bq).reshape(bs, n_ctx, HEADS, d)
        kv = (data @ Wkv + bkv).reshape(bs, n_data, HEADS, 2 * d)
        k, v = (kv[..., :d], kv[..., d:])
        scale = 1.0 / np.sqrt(d).astype(np.float32)
        scores = jnp.einsum('bqhd,bkhd->bhqk', q, k) * scale
        attn = jax.nn.softmax(scores, axis=-1)
        out = jnp.einsum('bhqk,bkhd->bqhd', attn, v).reshape(bs, n_ctx, WIDTH)
        return out @ Wp + bp

    def _L0_ffn_ref(x, ln_g, ln_b, router_w, eg, eb, W1, b1, W2, b2, Wo, bo):
        import jax, jax.numpy as jnp
        import numpy as np
        D, H, E, K = (256, 1024, 8, 2)
        B, T = (2, 512)

        def _layernorm(x, g, b, eps=1e-05):
            mu = jnp.mean(x, axis=-1, keepdims=True)
            var = jnp.mean(jnp.square(x - mu), axis=-1, keepdims=True)
            return (x - mu) * jax.lax.rsqrt(var + eps) * g + b

        def _expert(x, g, b, W1, b1, W2, b2, Wo, bo):
            x = _layernorm(x, g, b)
            x1 = x @ W1 + b1
            x2 = jnp.clip(x @ W2 + b2, -20.0, 20.0)
            hidden = jnp.clip(x1 * (x2 * jax.nn.sigmoid(x2)), -10000.0, 10000.0)
            return jnp.clip(hidden @ Wo + bo, -10000.0, 10000.0)
        Bb, Tt, Dd = x.shape
        xf = _layernorm(x.reshape(-1, Dd), ln_g, ln_b)
        N = xf.shape[0]
        logits = xf @ router_w
        scores, idx = jax.lax.top_k(logits, K)
        gate = jax.nn.softmax(scores, axis=-1)
        gates_e = jnp.zeros((N, E), xf.dtype).at[jnp.arange(N)[:, None], idx].add(gate)

        def body(acc, p):
            gcol, g, b, w1, bb1, w2, bb2, wo, bbo = p
            return (acc + gcol[:, None] * _expert(xf, g, b, w1, bb1, w2, bb2, wo, bbo), None)
        out, _ = jax.lax.scan(body, jnp.zeros_like(xf), (gates_e.T, eg, eb, W1, b1, W2, b2, Wo, bo))
        return out.reshape(Bb, Tt, Dd)
    x = x + _L0_xattn_ref(_layernorm(x, axis=-1), ctx_1024, L0_xattn_Wq, L0_xattn_bq, L0_xattn_Wkv, L0_xattn_bkv, L0_xattn_Wp, L0_xattn_bp)
    x = x + _L0_ffn_ref(_layernorm(x, axis=-1), L0_ffn_ln_g, L0_ffn_ln_b, L0_ffn_router_w, L0_ffn_eg, L0_ffn_eb, L0_ffn_W1, L0_ffn_b1, L0_ffn_W2, L0_ffn_b2, L0_ffn_Wo, L0_ffn_bo)
    return x

_drawn_inputs = setup_inputs


def setup_inputs(seed=0):
    import zlib

    import numpy as np

    out = dict(_drawn_inputs(seed))
    spreads = {'L0_xattn_bq': (0.0, 2.0),
     'L0_xattn_bkv': (0.0, 0.1),
     'L0_xattn_bp': (0.0, 0.1),
     'L0_ffn_ln_g': (1.0, 0.2),
     'L0_ffn_ln_b': (0.0, 0.327),
     'L0_ffn_eg': (1.0, 0.6),
     'L0_ffn_eb': (0.0, 0.8),
     'L0_ffn_b1': (0.0, 0.8),
     'L0_ffn_b2': (0.0, 0.8),
     'L0_ffn_bo': (0.0, 0.1)}
    factors = {'L0_xattn_Wq': 8.0}
    for name, (base, spread) in spreads.items():
        noise = np.random.default_rng([zlib.crc32(name.encode()), seed]).standard_normal(out[name].shape)
        drawn = base * np.exp(spread * noise) if base else spread * noise
        out[name] = jnp.asarray(drawn.astype(out[name].dtype))
    for name, factor in factors.items():
        out[name] = (out[name] * factor).astype(out[name].dtype)
    return out
```

```python
from contextlib import ExitStack

import numpy as np

import concourse.bass as bass
from concourse import mybir
from concourse.alu_op_type import AluOpType as ALU

F32 = mybir.dt.float32
F32R = mybir.dt.float32r
BF16 = mybir.dt.bfloat16
I32 = mybir.dt.int32
U32 = mybir.dt.uint32
ACTF = mybir.ActivationFunctionType
AXX = mybir.AxisListType.X

P = 128
BATCH, SEQ, D = 16, 256, 256
CTX = 77
HEADS, HD = 16, 16
EXPERTS, HIDDEN = 8, 1024
EPS = 1e-5
CLIP_OUT = 10000.0
CLIP_GATE = 20.0

TOKENS = BATCH * SEQ
NT = TOKENS // P
DC = D // P
HC = HIDDEN // P
HPC = HEADS // DC
KEYS = HEADS * CTX
KB = -(-KEYS // P)
TAIL = KEYS - (KB - 1) * P
BLOCK_HEADS = 3
VW = HD + 1

TILE = 512
SUBS = TILE // P
MAX_TILES = (2 * TOKENS + EXPERTS * (TILE - 1)) // TILE
SLOT_BLOCKS = MAX_TILES * SUBS
ROWS = TOKENS + P

C_IDENT = 0
C_TRI = C_IDENT + P
C_IOTA = C_TRI + P
C_KMASK = C_IOTA + P
C_VMASK = C_KMASK + HPC
C_TOKEN = C_VMASK + KB * BLOCK_HEADS
C_DUMP = C_TOKEN + NT
C_THR = C_DUMP + 1
NTHR = -(-TOKENS // TILE)
C_END = C_THR + NTHR

X_G, X_B, X_B1, X_B2 = 0, DC, 2 * DC, 2 * DC + HC
X_END = 2 * DC + 2 * HC


def block_heads(i):
    first = i * P // CTX
    last = min(i * P + P - 1, KEYS - 1) // CTX
    return first, last - first + 1


def constants():
    c = np.zeros((P, C_END), np.float32)
    p = np.arange(P)
    c[:, C_IDENT:C_IDENT + P] = np.eye(P)
    c[:, C_TRI:C_TRI + P] = p[:, None] < p[None, :]
    c[:, C_IOTA:C_IOTA + P] = p[None, :]
    c[:, C_KMASK:C_KMASK + HPC] = (p[:, None] // HD) == np.arange(HPC)[None, :]
    for i in range(KB):
        first, n = block_heads(i)
        for j in range(BLOCK_HEADS):
            c[:, C_VMASK + i * BLOCK_HEADS + j] = (i * P + p) // CTX == first + j
    c[:, C_TOKEN:C_TOKEN + NT] = 1 + p[:, None] + P * np.arange(NT)[None, :]
    c[:, C_DUMP] = TOKENS + 1 + p
    c[:, C_THR:C_THR + NTHR] = TILE * np.arange(NTHR)[None, :]
    return c


class Queue:

    def __init__(self, sem):
        self.sem, self.count, self.items, self.reached = sem, 0, [], {}

    def do(self, fn):
        self.items.append(fn)

    def sig(self, fn):
        self.count += 1
        self.items.append(lambda e: fn(e).then_inc(self.sem, 1))
        return self.sem, self.count

    def wait(self, *tokens):
        for sem, value in tokens:
            if self.reached.get(id(sem), 0) < value:
                self.reached[id(sem)] = value
                self.items.append(lambda e, sem=sem, value=value: e.wait_ge(sem, value))

    def then(self, fn):
        token = self.sig(fn)
        self.wait(token)
        return token

    def dma(self, flow, out, in_):
        flow.count += 16
        self.items.append(lambda e: e.dma_start(out, in_).then_inc(flow.sem, 16))
        return flow.sem, flow.count

    def emit(self, engine):
        for item in self.items:
            item(engine)


class Flow:

    def __init__(self, sem):
        self.sem, self.count = sem, 0

    @property
    def token(self):
        return self.sem, self.count


def build(nc, a, out):
    ctx = ExitStack()

    scope = [ctx]

    def sb(name, shape, dt=F32):
        return scope[-1].enter_context(nc.sbuf_tensor(name, shape, dt))

    def sem(name):
        return ctx.enter_context(nc.semaphore(name))

    def flow(name):
        return Flow(sem(name))

    PR = 3
    with ctx:
        z_rows = nc.dram_tensor("z_rows", [ROWS, D], F32, kind="Internal").ap()
        v_flat = nc.dram_tensor("v_flat", [BATCH, KEYS, VW], F32, kind="Internal").ap()

        pe, act, dve, pool, sp = (Queue(sem(n)) for n in
                                  ("pe_done", "act_done", "dve_done", "pool_done", "sp_done"))
        f_const, f_weights = flow("f_const"), flow("f_weights")
        f_x = [flow(f"f_x{i}") for i in range(6)]
        f_ctx = [flow(f"f_ctx{i}") for i in range(2)]
        f_vstore = [flow(f"f_vstore{i}") for i in range(2)]
        f_vload = [flow(f"f_vload{i}") for i in range(2)]
        f_x1 = [flow(f"f_x1_{i}") for i in range(3)]
        f_z = [flow(f"f_z{i}") for i in range(3)]
        f_dump = flow("f_dump")
        f_raw = [flow(f"f_raw{i}") for i in range(3)]
        f_par = [flow(f"f_par{i}") for i in range(PR)]
        f_gather = [flow(f"f_gather{i}") for i in range(2)]
        f_scatter = flow("f_scatter")

        banks = [ctx.enter_context(nc.psum_tensor(f"bank{i}", [P, 512], F32)) for i in range(8)]

        const = sb("const", [P, C_END])
        ident = const[:, C_IDENT:C_IDENT + P]
        wq, wk, wv, wp = (sb(n, [P, DC, D]) for n in ("wq", "wk", "wv", "wp"))
        router = sb("router", [P, DC, EXPERTS])
        qk_bias = sb("qk_bias", [P, 2 * DC])
        rows = sb("rows", [P, 4, D])
        bv_row, bp_row, g_row, b_row = (rows[:, i, :] for i in range(4))
        half = sb("half", [P, 1])
        zeros = sb("zeros", [P, D])

        sp.dma(f_const, const[:, :], a["const"])
        sp.dma(f_const, qk_bias[:, :], a["qk_bias"])
        for i, n in enumerate(("bv", "bp", "ln_g", "ln_b")):
            sp.dma(f_const, rows[:, i, :], a[n].broadcast_to([P, D]))
        t_const = f_const.token

        logits = sb("logits", [P, NT, EXPERTS])

        scope.append(ExitStack())
        XR = 6
        xs = [sb(f"xs{i}", [P, D]) for i in range(XR)]
        cs = [sb(f"cs{i}", [CTX, D]) for i in range(2)]
        c_t = sb("c_t", [P, DC, CTX])
        k_t = sb("k_t", [P, DC, CTX])
        k_blocks = [sb(f"k_blocks{i}", [P, DC, HPC, CTX]) for i in range(2)]
        v_sb = [sb(f"v_sb{i}", [CTX, HEADS, VW]) for i in range(2)]
        v_rep = [sb(f"v_rep{i}", [P, KB, VW]) for i in range(2)]
        v_blocks = [sb(f"v_blocks{i}", [P, KB, BLOCK_HEADS, VW]) for i in range(2)]
        xn = [sb(f"xn{i}", [P, D]) for i in range(2)]
        xn_t = [sb(f"xn_t{i}", [P, DC, SEQ]) for i in range(2)]
        q_t = [sb(f"q_t{i}", [P, DC, SEQ]) for i in range(2)]
        probs = [sb(f"probs{i}", [P, HEADS, CTX]) for i in range(2)]
        probs_t = [sb(f"probs_t{i}", [P, KB, P]) for i in range(2)]
        attn = [sb(f"attn{i}", [P, D]) for i in range(2)]
        attn_t = [sb(f"attn_t{i}", [P, DC, P]) for i in range(2)]
        xb = [sb(f"xb{i}", [P, D]) for i in range(4)]
        x1 = [sb(f"x1_{i}", [P, D]) for i in range(3)]
        y = [sb(f"y{i}", [P, D]) for i in range(2)]
        xf = [sb(f"xf{i}", [P, D]) for i in range(2)]
        xf_t = [sb(f"xf_t{i}", [P, DC, P]) for i in range(2)]
        z = [sb(f"z{i}", [P, D]) for i in range(3)]
        small = sb("small", [P, 4, 16])
        maxes = [sb(f"maxes{i}", [P, HEADS]) for i in range(2)]
        recip = [sb(f"recip{i}", [P, HEADS]) for i in range(2)]
        stats = sb("stats", [P, 3, 4, 6])

        score_bank = banks[0:3]
        trans_bank = banks[3:5]
        value_bank = banks[5]
        misc_bank = banks[6:8]
        score_free = [None] * 3
        trans_free = [None] * 2
        value_free = None
        misc_free = [None, None]
        turn = {"misc": 0, "score": 0, "trans": 0}

        def take(kind, free, queue):
            n = turn[kind] % len(free)
            turn[kind] += 1
            if free[n]:
                queue.wait(free[n])
            return n

        t = {}

        t_half = pool.sig(lambda e: e.memset(half[:, :], -0.5))
        t_zero = pool.sig(lambda e: e.memset(zeros[:, :], 0.0))
        t_ones = [pool.sig(lambda e, i=i: e.memset(v_sb[i][:, :, HD:VW], 1.0)) for i in range(2)]

        def load_x(i):
            if i >= XR:
                sp.wait(t["xb", i - XR], t["xn", i - XR])
            t["x", i] = sp.dma(f_x[i % XR], xs[i % XR][:, :], a["x"][i * P:(i + 1) * P, :])

        def load_ctx(b):
            if b >= 2:
                sp.wait(t["ctx_t", b - 2])
            t["ctx", b] = sp.dma(f_ctx[b % 2], cs[b % 2][:, :], a["ctx"][b * CTX:(b + 1) * CTX, :])

        def rsqrt_on_pool(dst, src):
            pool.then(lambda e: e.tensor_scalar(dst, src, EPS, None, ALU.add))
            return pool.then(lambda e: e.tensor_tensor(dst, dst, half[:, :], ALU.pow))

        def norm_stats(which, i, src):
            st = stats[:, which, i % 4, :]
            mv = small[:, i % 4, 4 * which:4 * which + 2]
            dve.then(lambda e: e.bn_stats(st, src))
            return dve.sig(lambda e: e.bn_aggr(mv, st))

        def keys_values(b):
            n = take("misc", misc_free, pe)
            pe.wait(t["ctx", b], t_const)
            ps = misc_bank[n]
            for c in range(DC):
                tok = pe.sig(lambda e, c=c: e.transpose(ps[:, c * CTX:(c + 1) * CTX],
                                                        cs[b % 2][:, c * P:(c + 1) * P],
                                                        ident[0:CTX, 0:CTX]))
            t["ctx_t", b] = tok
            act.wait(tok)
            if b:
                act.wait(t["kv_mm", b - 1])
            tok = act.sig(lambda e: e.activation(c_t[:, :, :], ps[:, 0:DC * CTX].rearrange(
                "p (c k) -> p c k", c=DC), ACTF.Copy))
            misc_free[n] = tok
            n = take("misc", misc_free, pe)
            pe.wait(tok, t_weights)
            psk = misc_bank[n]
            for m in range(DC):
                for c in range(DC):
                    tk = pe.sig(lambda e, m=m, c=c: e.matmul(
                        psk[:, m * CTX:(m + 1) * CTX], wk[:, c, m * P:(m + 1) * P], c_t[:, c, :],
                        start=(c == 0), stop=(c == DC - 1)))
            nv = take("misc", misc_free, pe)
            psv = misc_bank[nv]
            for c in range(DC):
                tv = pe.sig(lambda e, c=c: e.matmul(psv[0:CTX, 0:D], c_t[:, c, :], wv[:, c, :],
                                                    start=(c == 0), stop=(c == DC - 1)))
            t["kv_mm", b] = tv
            act.wait(tk, t_const)
            if b:
                act.wait(t["k_blocks", b - 1])
            for m in range(DC):
                tok = act.sig(lambda e, m=m: e.activation(
                    k_t[:, m, :], psk[:, m * CTX:(m + 1) * CTX], ACTF.Identity,
                    bias=qk_bias[:, DC + m:DC + m + 1]))
            misc_free[n] = tok
            pool.wait(tok)
            if b >= 2:
                pool.wait(t["scores", 2 * (b - 2) + 1])
            for m in range(DC):
                tok = pool.sig(lambda e, m=m: e.tensor_tensor(
                    k_blocks[b % 2][:, m, :, :],
                    k_t[:, m, :].unsqueeze(1).broadcast_to([P, HPC, CTX]),
                    const[:, C_KMASK:C_KMASK + HPC].unsqueeze(2).broadcast_to([P, HPC, CTX]),
                    ALU.mult))
            t["k_blocks", b] = tok
            dve.wait(tv, t_const, t_ones[1])
            if b >= 2:
                dve.wait(t["v_store", b - 2])
            tok = dve.sig(lambda e: e.tensor_tensor(
                v_sb[b % 2][:, :, 0:HD],
                psv[0:CTX, 0:D].rearrange("k (h d) -> k h d", h=HEADS),
                bv_row[0:CTX, :].rearrange("k (h d) -> k h d", h=HEADS), ALU.add))
            misc_free[nv] = tok
            sp.wait(tok)
            t["v_store", b] = sp.dma(f_vstore[b % 2],
                                     v_flat[b].rearrange("(h k) d -> k h d", h=HEADS),
                                     v_sb[b % 2][:, :, :])

        def load_values(b):
            sp.wait(t["v_store", b])
            if b >= 2:
                sp.wait(t["v_blocks", b - 2])
            full = (KB - 1) * P
            sp.dma(f_vload[b % 2], v_rep[b % 2][:, 0:KB - 1, :],
                   v_flat[b][0:full, :].rearrange("(i p) d -> p i d", p=P))
            t["v_load", b] = sp.dma(f_vload[b % 2], v_rep[b % 2][0:TAIL, KB - 1, :],
                                    v_flat[b][full:KEYS, :])

        def spread_values(b):
            pool.wait(t["v_load", b], t_const)
            if b >= 2:
                pool.wait(t["values", 2 * (b - 2) + 1])
            vm = const[:, C_VMASK:C_VMASK + KB * BLOCK_HEADS].rearrange(
                "p (i j) -> p i j", i=KB)
            for j in range(BLOCK_HEADS):
                for parts, lo, hi in ((P, 0, KB - 1), (TAIL, KB - 1, KB)):
                    tok = pool.sig(lambda e, j=j, parts=parts, lo=lo, hi=hi: e.tensor_tensor(
                        v_blocks[b % 2][0:parts, lo:hi, j, :], v_rep[b % 2][0:parts, lo:hi, :],
                        vm[0:parts, lo:hi, j:j + 1].broadcast_to([parts, hi - lo, VW]),
                        ALU.mult))
            t["v_blocks", b] = tok

        def norm_x(i):
            dve.wait(t["x", i])
            src = xs[i % XR]
            tok = norm_stats(0, i, src[:, :])
            pool.wait(tok, t_half)
            sm = small[:, i % 4, :]
            tok = rsqrt_on_pool(sm[:, 2:3], sm[:, 1:2])
            dve.wait(tok)
            if i >= 2:
                dve.wait(t["xn_t", i - 2])
            t["xn", i] = dve.sig(lambda e: e.tensor_scalar(
                xn[i % 2][:, :], src[:, :], sm[:, 0:1], sm[:, 2:3], ALU.subtract, ALU.mult))
            pool.wait(t_const)
            if i >= 4:
                pool.wait(t["x1", i - 4])
            t["xb", i] = pool.sig(lambda e: e.tensor_tensor(
                xb[i % 4][:, :], src[:, :], bp_row, ALU.add))

        def transpose_xn(i):
            b, s = divmod(i, 2)
            n = take("misc", misc_free, pe)
            ps = misc_bank[n]
            pe.wait(t["xn", i], t_const)
            for c in range(DC):
                tok = pe.sig(lambda e, c=c: e.transpose(
                    ps[:, c * P:(c + 1) * P], xn[i % 2][:, c * P:(c + 1) * P], ident))
            t["xn_t", i] = tok
            act.wait(tok)
            if b >= 2:
                act.wait(t["q_mm", b - 2])
            tok = act.sig(lambda e: e.activation(
                xn_t[b % 2][:, :, s * P:(s + 1) * P],
                ps[:, 0:DC * P].rearrange("p (c k) -> p c k", c=DC), ACTF.Copy))
            misc_free[n] = tok
            t["xn_t_sb", i] = tok

        def queries(b):
            n = take("misc", misc_free, pe)
            ps = misc_bank[n]
            pe.wait(t["xn_t_sb", 2 * b + 1], t_weights)
            for m in range(DC):
                for c in range(DC):
                    tok = pe.sig(lambda e, m=m, c=c: e.matmul(
                        ps[:, m * SEQ:(m + 1) * SEQ], wq[:, c, m * P:(m + 1) * P],
                        xn_t[b % 2][:, c, :], start=(c == 0), stop=(c == DC - 1)))
            t["q_mm", b] = tok
            dve.wait(tok)
            if b >= 2:
                dve.wait(t["scores", 2 * (b - 2) + 1])
            for m in range(DC):
                tok = dve.sig(lambda e, m=m: e.tensor_scalar(
                    q_t[b % 2][:, m, :], ps[:, m * SEQ:(m + 1) * SEQ], qk_bias[:, m:m + 1],
                    1.0 / float(np.sqrt(HD)), ALU.add, ALU.mult))
            misc_free[n] = tok
            t["q", b] = tok

        HPB = HPC // 2

        def scores(i, u):
            b, s = divmod(i, 2)
            m, g = divmod(u, 2)
            n = take("score", score_free, pe)
            ps = score_bank[n]
            pe.wait(t["q", b], t["k_blocks", b])
            tok = pe.sig(lambda e: e.matmul(
                ps[:, 0:HPB * CTX], q_t[b % 2][:, m, s * P:(s + 1) * P],
                k_blocks[b % 2][:, m, g * HPB:(g + 1) * HPB, :].rearrange("p h k -> p (h k)"),
                start=True, stop=True))
            t["scores", i] = tok
            h0 = u * HPB
            view = ps[:, 0:HPB * CTX].rearrange("p (h k) -> p h k", h=HPB)
            mx = maxes[i % 2][:, h0:h0 + HPB]
            dve.wait(tok)
            if u == 0 and i >= 2:
                dve.wait(t["probs_t", i - 2])
            dve.then(lambda e: e.tensor_reduce(mx, view, AXX, ALU.max))
            tok = dve.sig(lambda e: e.tensor_tensor(
                probs[i % 2][:, h0:h0 + HPB, :], view,
                mx.unsqueeze(2).broadcast_to([P, HPB, CTX]), ALU.subtract))
            score_free[n] = tok
            if g == 1:
                act.wait(tok)
                part = probs[i % 2][:, m * HPC:(m + 1) * HPC, :]
                t["probs", i, m] = act.sig(lambda e: e.activation(part, part, ACTF.Exp))

        def transpose_probs(i, g):
            n = take("trans", trans_free, pe)
            ps = trans_bank[n]
            flat = probs[i % 2][:, :, :].rearrange("p h k -> p (h k)")
            blocks = list(range(4 * g, min(4 * g + 4, KB)))
            pe.wait(t["probs", i, 0 if (blocks[-1] + 1) * P <= HPC * CTX else 1])
            for j, k in enumerate(blocks):
                size = P if k < KB - 1 else TAIL
                tok = pe.sig(lambda e, j=j, k=k, size=size: e.transpose(
                    ps[0:size, j * P:(j + 1) * P], flat[:, k * P:k * P + size], ident))
            t["probs_t", i] = tok
            queue = (act, dve, act)[g]
            queue.wait(tok)
            if i >= 2:
                queue.wait(t["values", i - 2])
            whole = [k for k in blocks if k < KB - 1]
            pieces = [(P, 0, len(whole))] + ([(TAIL, len(whole), len(blocks))]
                                             if len(whole) < len(blocks) else [])
            for parts, lo, hi in pieces:
                dst = probs_t[i % 2][0:parts, blocks[0] + lo:blocks[0] + hi, :]
                src = ps[0:parts, lo * P:hi * P].rearrange("p (j k) -> p j k", k=P)
                if queue is act:
                    tok = act.sig(lambda e, dst=dst, src=src: e.activation(dst, src, ACTF.Copy))
                else:
                    tok = dve.sig(lambda e, dst=dst, src=src: e.tensor_copy(dst, src))
            trans_free[n] = tok
            t["probs_t_sb", i, g] = tok

        def values(i):
            nonlocal value_free
            b = i // 2
            if value_free:
                pe.wait(value_free)
            pe.wait(t["v_blocks", b])
            for k in range(KB):
                if k % 4 == 0:
                    pe.wait(t["probs_t_sb", i, k // 4])
                first, nh = block_heads(k)
                size = P if k < KB - 1 else TAIL
                tok = pe.sig(lambda e, k=k, first=first, nh=nh, size=size: e.matmul(
                    value_bank[:, first * VW:(first + nh) * VW],
                    probs_t[i % 2][0:size, k, :],
                    v_blocks[b % 2][0:size, k, 0:nh, :].rearrange("p j d -> p (j d)"),
                    start=(k == 0), stop=(k == KB - 1), skip_group_check=True))
            t["values", i] = tok
            dve.wait(tok)
            view = value_bank[:, 0:HEADS * VW].rearrange("p (h d) -> p h d", h=HEADS)
            dve.then(lambda e: e.reciprocal(recip[i % 2][:, :].unsqueeze(2), view[:, :, HD:VW]))
            if i >= 2:
                dve.wait(t["attn_t", i - 2])
            tok = dve.sig(lambda e: e.tensor_tensor(
                attn[i % 2][:, :].rearrange("p (h d) -> p h d", h=HEADS), view[:, :, 0:HD],
                recip[i % 2][:, :].unsqueeze(2).broadcast_to([P, HEADS, HD]), ALU.mult))
            value_free = tok
            t["attn", i] = tok

        def transposed_tile(i, src, src_token, dst, dst_readers, name):
            n = take("misc", misc_free, pe)
            ps = misc_bank[n]
            pe.wait(src_token)
            for c in range(DC):
                tok = pe.sig(lambda e, c=c: e.transpose(
                    ps[:, c * P:(c + 1) * P], src[:, c * P:(c + 1) * P], ident))
            t[name, i] = tok
            act.wait(tok, *dst_readers)
            tok = act.sig(lambda e: e.activation(
                dst[:, :, :], ps[:, 0:DC * P].rearrange("p (c k) -> p c k", c=DC), ACTF.Copy))
            misc_free[n] = tok
            return tok

        def transpose_attn(i):
            t["attn_t_sb", i] = transposed_tile(
                i, attn[i % 2], t["attn", i], attn_t[i % 2],
                [t["proj", i - 2]] if i >= 2 else [], "attn_t")

        def project(i):
            n = take("misc", misc_free, pe)
            ps = misc_bank[n]
            pe.wait(t["attn_t_sb", i], t_weights)
            for c in range(DC):
                tok = pe.sig(lambda e, c=c: e.matmul(ps[:, 0:D], attn_t[i % 2][:, c, :],
                                                     wp[:, c, :], start=(c == 0),
                                                     stop=(c == DC - 1)))
            t["proj", i] = tok
            dve.wait(tok, t["xb", i])
            if i >= 3:
                dve.wait(t["x1_store", i - 3])
            tok = dve.sig(lambda e: e.tensor_tensor(x1[i % 3][:, :], ps[:, 0:D], xb[i % 4][:, :],
                                                    ALU.add))
            misc_free[n] = tok
            t["x1", i] = tok
            sp.wait(tok)
            t["x1_store", i] = sp.dma(f_x1[i % 3], out[i * P:(i + 1) * P, :], x1[i % 3][:, :])

            dve.wait(tok)
            tok = norm_stats(1, i, x1[i % 3][:, :])
            pool.wait(tok)
            sm = small[:, i % 4, :]
            r1, r2 = sm[:, 12:13], sm[:, 13:14]
            rsqrt_on_pool(r1, sm[:, 5:6])
            pool.then(lambda e: e.tensor_tensor(r2, r1, r1, ALU.mult))
            pool.then(lambda e: e.tensor_tensor(r2, r2, sm[:, 5:6], ALU.mult))
            rsqrt_on_pool(r2, r2)
            tok = pool.sig(lambda e: e.tensor_tensor(sm[:, 6:7], r1, r2, ALU.mult))
            dve.wait(tok)
            if i >= 2:
                dve.wait(t["xf", i - 2])
            tok = dve.sig(lambda e: e.tensor_scalar(y[i % 2][:, :], x1[i % 3][:, :], sm[:, 4:5],
                                                    sm[:, 6:7], ALU.subtract, ALU.mult))
            pool.wait(tok)
            if i >= 2:
                pool.wait(t["xf_t", i - 2], t["z", i - 2])
            pool.then(lambda e: e.tensor_tensor(xf[i % 2][:, :], y[i % 2][:, :], g_row, ALU.mult))
            t["xf", i] = pool.sig(lambda e: e.tensor_tensor(xf[i % 2][:, :], xf[i % 2][:, :],
                                                            b_row, ALU.add))

        def finish_norm(i):
            sm = small[:, i % 4, :]
            dve.wait(t["xf", i])
            tok = norm_stats(2, i, xf[i % 2][:, :])
            pool.wait(tok)
            tok = rsqrt_on_pool(sm[:, 10:11], sm[:, 9:10])
            dve.wait(tok)
            if i >= 3:
                dve.wait(t["z_store", i - 3])
            tok = dve.sig(lambda e: e.tensor_scalar(z[i % 3][:, :], xf[i % 2][:, :], sm[:, 8:9],
                                                    sm[:, 10:11], ALU.subtract, ALU.mult))
            t["z", i] = tok
            sp.wait(tok)
            t["z_store", i] = sp.dma(f_z[i % 3], z_rows[i * P:(i + 1) * P, :], z[i % 3][:, :])

        def route_logits(i):
            tok = transposed_tile(i, xf[i % 2], t["xf", i], xf_t[i % 2],
                                  [t["logits_mm", i - 2]] if i >= 2 else [], "xf_t")
            n = take("misc", misc_free, pe)
            ps = misc_bank[n]
            pe.wait(tok, t_weights)
            for c in range(DC):
                tok = pe.sig(lambda e, c=c: e.matmul(ps[:, 0:EXPERTS], xf_t[i % 2][:, c, :],
                                                     router[:, c, :], start=(c == 0),
                                                     stop=(c == DC - 1)))
            t["logits_mm", i] = tok
            act.wait(tok)
            tok = act.sig(lambda e: e.activation(logits[:, i, :], ps[:, 0:EXPERTS], ACTF.Copy))
            misc_free[n] = tok
            t["logits", i] = tok

        for i in range(XR):
            load_x(i)
        load_ctx(0)
        for dst, n in ((wk, "wk"), (wv, "wv"), (wq, "wq"), (wp, "wp"), (router, "router")):
            sp.dma(f_weights, dst[:, :, :], a[n].rearrange("(c p) n -> p c n", p=P))
        t_weights = f_weights.token
        load_ctx(1)
        sp.wait(t_zero)
        sp.dma(f_dump, z_rows[TOKENS:ROWS, :], zeros[:, :])
        sp.dma(f_dump, out[TOKENS:ROWS, :], zeros[:, :])

        keys_values(0)
        for i in range(2):
            norm_x(i)
            transpose_xn(i)
        queries(0)
        load_values(0)
        spread_values(0)

        for i in range(NT + 3):
            b, s = divmod(i, 2)
            if XR <= i + XR - 2 < NT:
                load_x(i + XR - 2)
            nb = b + 1
            if i < NT:
                scores(i, 0)
                scores(i, 1)
            if 1 <= i <= NT:
                transpose_probs(i - 1, 0)
            if i < NT:
                scores(i, 2)
            if 2 <= i < NT + 2:
                transpose_attn(i - 2)
            if 1 <= i <= NT:
                transpose_probs(i - 1, 1)
            if i < NT:
                scores(i, 3)
            if 2 <= i < NT + 2:
                project(i - 2)
            if 1 <= i <= NT:
                transpose_probs(i - 1, 2)
            if i < NT and nb < BATCH:
                if s == 0:
                    keys_values(nb)
                    if nb + 1 < BATCH:
                        load_ctx(nb + 1)
                norm_x(2 * nb + s)
                transpose_xn(2 * nb + s)
                if s == 1:
                    load_values(nb)
                    spread_values(nb)
            if 1 <= i <= NT:
                values(i - 1)
            if i < NT and nb < BATCH and s == 1:
                queries(nb)
            if i >= 3:
                route_logits(i - 3)
            if 2 <= i < NT + 2:
                finish_norm(i - 2)

        scope.pop().close()
        stage1_stores = [t[n, i] for n in ("x1_store", "z_store") for i in range(NT - 3, NT)]

        best = sb("best", [P, NT, 8])
        best_idx = sb("best_idx", [P, NT, 8], U32)
        pick = sb("pick", [P, 2, NT])
        gates = sb("gates", [P, 2, NT])
        gate_sum = sb("gate_sum", [P, NT])
        chosen = sb("chosen", [P, 2, NT, EXPERTS])
        both = sb("both", [P, NT, EXPERTS], BF16)
        tri = sb("tri", [P, P], BF16)
        ones = sb("ones", [P, P], BF16)
        totals = sb("totals", [P, NT, EXPERTS])
        running = sb("running", [P, EXPERTS, NT])
        zero8 = sb("zero8", [P, NT])
        place = sb("place", [P, NT, EXPERTS])
        over = sb("over", [P, EXPERTS, NTHR])
        n_tiles = sb("n_tiles", [P, EXPERTS])
        tile_end = sb("tile_end", [P, EXPERTS])
        tile_start = sb("tile_start", [P, EXPERTS])
        base = sb("base", [P, EXPERTS])
        begun = sb("begun", [1, MAX_TILES, EXPERTS])
        tile_expert_f = sb("tile_expert_f", [1, MAX_TILES])
        tile_expert = sb("tile_expert", [1, MAX_TILES], I32)
        slot = sb("slot", [P, 2, NT])
        slot_i = sb("slot_i", [P, 2, NT], I32)
        hi_lo_i = sb("hi_lo_i", [P, 2, 2, NT], I32)
        hi_lo = sb("hi_lo", [P, 2, 2, NT])
        AR = 4
        at_lo = [sb(f"at_lo{i}", [P, P]) for i in range(AR)]
        at_hi = [sb(f"at_hi{i}", [P, 2, SLOT_BLOCKS]) for i in range(AR)]
        filled = sb("filled", [P, 2, SLOT_BLOCKS])
        dump = sb("dump", [P, SLOT_BLOCKS])
        row_of = sb("row_of", [P, SLOT_BLOCKS], I32)

        iota = const[:, C_IOTA:C_IOTA + P]
        dve.wait(t_const)
        dve.sig(lambda e: e.tensor_copy(tri[:, :], const[:, C_TRI:C_TRI + P]))
        dve.sig(lambda e: e.memset(ones[:, :], 1.0))
        dve.sig(lambda e: e.memset(zero8[:, :], 0.0))
        dve.wait(t["logits", NT - 1])
        for i in range(NT):
            tok = dve.sig(lambda e, i=i: e.max(best[:, i, :], logits[:, i, :]))
        dve.wait(tok)
        for i in range(NT):
            tok = dve.sig(lambda e, i=i: e.max_index(best_idx[:, i, :], best[:, i, :],
                                                     logits[:, i, :]))
        tok2 = dve.then(lambda e: e.tensor_tensor(gates[:, 1, :], best[:, :, 1], best[:, :, 0],
                                                  ALU.subtract))
        act.wait(tok2)
        tok2 = act.sig(lambda e: e.activation(gates[:, 1, :], gates[:, 1, :], ACTF.Exp))
        dve.then(lambda e: e.tensor_copy(pick[:, :, :], best_idx[:, :, 0:2].rearrange(
            "p t k -> p k t")))
        for k in range(2):
            tok = dve.sig(lambda e, k=k: e.tensor_tensor(
                chosen[:, k, :, :], pick[:, k, :].unsqueeze(2).broadcast_to([P, NT, EXPERTS]),
                iota[:, 0:EXPERTS].unsqueeze(1).broadcast_to([P, NT, EXPERTS]), ALU.is_equal))
        dve.wait(tok)
        tok = dve.sig(lambda e: e.tensor_tensor(both[:, :, :], chosen[:, 0, :, :],
                                                chosen[:, 1, :, :], ALU.add))
        pe.wait(tok)
        pe.wait(*[f for f in score_free if f])
        flat_both = both[:, :, :].rearrange("p t e -> p (t e)")
        nte = NT * EXPERTS
        tok_pre = pe.sig(lambda e: e.matmul(banks[0][:, 0:nte], tri[:, :], flat_both, start=True,
                                            stop=True))
        tok_tot = pe.sig(lambda e: e.matmul(banks[1][:, 0:nte], ones[:, :], flat_both, start=True,
                                            stop=True))
        dve.wait(tok2)
        dve.then(lambda e: e.tensor_scalar(gate_sum[:, :], gates[:, 1, :], 1.0, None, ALU.add))
        dve.then(lambda e: e.reciprocal(gates[:, 0, :], gate_sum[:, :]))
        dve.then(lambda e: e.tensor_tensor(gates[:, 1, :], gates[:, 1, :], gates[:, 0, :],
                                           ALU.mult))
        dve.wait(tok_tot)
        dve.then(lambda e: e.tensor_copy(totals[:, :, :], banks[1][:, 0:nte].rearrange(
            "p (t e) -> p t e", t=NT)))
        for x in range(EXPERTS):
            tok = dve.sig(lambda e, x=x: e.tensor_tensor_scan(
                running[:, x, :], totals[:, :, x], zero8[:, :], 0.0, ALU.add, ALU.add))
        dve.wait(tok)
        dve.then(lambda e: e.tensor_tensor(
            over[:, :, :], running[:, :, NT - 1:NT].broadcast_to([P, EXPERTS, NTHR]),
            const[:, C_THR:C_THR + NTHR].unsqueeze(1).broadcast_to([P, EXPERTS, NTHR]),
            ALU.is_gt))
        dve.then(lambda e: e.tensor_reduce(n_tiles[:, :], over[:, :, :], AXX, ALU.add))
        dve.then(lambda e: e.tensor_tensor_scan(tile_end[:, :], n_tiles[:, :],
                                                zero8[:, 0:EXPERTS], 0.0, ALU.add, ALU.add))
        dve.then(lambda e: e.tensor_tensor(tile_start[:, :], tile_end[:, :], n_tiles[:, :],
                                           ALU.subtract))
        dve.then(lambda e: e.tensor_scalar(base[:, :], tile_start[:, :], float(TILE), None,
                                           ALU.mult))
        dve.then(lambda e: e.tensor_tensor(
            begun[:, :, :],
            tile_start[0:1, :].unsqueeze(1).broadcast_to([1, MAX_TILES, EXPERTS]),
            iota[0:1, 0:MAX_TILES].unsqueeze(2).broadcast_to([1, MAX_TILES, EXPERTS]),
            ALU.is_le))
        dve.then(lambda e: e.tensor_reduce(tile_expert_f[:, :], begun[:, :, :], AXX, ALU.add))
        t_tile_expert = dve.sig(lambda e: e.tensor_scalar(
            tile_expert[:, :], tile_expert_f[:, :], -1.0, None, ALU.add))
        dve.wait(tok_pre)
        dve.then(lambda e: e.tensor_tensor(
            place[:, :, :], banks[0][:, 0:nte].rearrange("p (t e) -> p t e", t=NT),
            running[:, :, :].rearrange("p e t -> p t e"), ALU.add))
        dve.then(lambda e: e.tensor_tensor(place[:, :, :], place[:, :, :], totals[:, :, :],
                                           ALU.subtract))
        dve.then(lambda e: e.tensor_tensor(
            place[:, :, :], place[:, :, :],
            base[:, :].unsqueeze(1).broadcast_to([P, NT, EXPERTS]), ALU.add))
        for k in range(2):
            dve.then(lambda e, k=k: e.tensor_tensor(chosen[:, k, :, :], chosen[:, k, :, :],
                                                    place[:, :, :], ALU.mult))
            tok = dve.sig(lambda e, k=k: e.tensor_reduce(slot[:, k, :], chosen[:, k, :, :], AXX,
                                                         ALU.add))
        dve.wait(tok)
        dve.then(lambda e: e.tensor_copy(slot_i[:, :, :], slot[:, :, :]))
        dve.sig(lambda e: e.tensor_single_scalar(hi_lo_i[:, 0, :, :], slot_i[:, :, :], 7,
                                                 ALU.logical_shift_right))
        dve.then(lambda e: e.tensor_single_scalar(hi_lo_i[:, 1, :, :], slot_i[:, :, :], P - 1,
                                                  ALU.bitwise_and))
        dve.then(lambda e: e.tensor_copy(hi_lo[:, :, :, :], hi_lo_i[:, :, :, :]))
        fill_bank = banks[2]
        used = []
        for n in range(2 * NT):
            k, i = divmod(n, NT)
            if n >= AR:
                dve.wait(used[n - AR])
            lo, hi = hi_lo[:, 1, k, i:i + 1], hi_lo[:, 0, k, i:i + 1]
            dve.sig(lambda e, n=n, lo=lo: e.tensor_scalar(at_lo[n % AR][:, :], iota, lo, None,
                                                          ALU.is_equal))
            for w, value in enumerate((const[:, C_TOKEN + i:C_TOKEN + i + 1],
                                       gates[:, k, i:i + 1])):
                tok = dve.sig(lambda e, n=n, hi=hi, w=w, value=value: e.tensor_scalar(
                    at_hi[n % AR][:, w, :], iota[:, 0:SLOT_BLOCKS], hi, value, ALU.is_equal,
                    ALU.mult))
            pe.wait(tok)
            used.append(pe.sig(lambda e, n=n: e.matmul(
                fill_bank[:, 0:2 * SLOT_BLOCKS], at_lo[n % AR][:, :],
                at_hi[n % AR][:, :, :].rearrange("p w s -> p (w s)"), start=(n == 0),
                stop=(n == 2 * NT - 1))))
        dve.wait(used[-1])
        t_gate = dve.then(lambda e: e.tensor_copy(filled[:, :, :], fill_bank[
            :, 0:2 * SLOT_BLOCKS].rearrange("p (w s) -> p w s", w=2)))
        dve.then(lambda e: e.tensor_scalar(dump[:, :], filled[:, 0, :], 0.0,
                                           const[:, C_DUMP:C_DUMP + 1], ALU.is_equal, ALU.mult))
        t_rows = dve.sig(lambda e: e.scalar_tensor_tensor(
            row_of[:, :], filled[:, 0, :], -1.0, dump[:, :], ALU.add, ALU.add))

        raw = [sb(f"raw{i}", [P, 2, HIDDEN]) for i in range(3)]
        wh = [sb(f"wh{i}", [P, 3, 2, HIDDEN], F32R) for i in range(2)]
        wl = [sb(f"wl{i}", [P, 3, 2, HIDDEN], F32R) for i in range(2)]
        par = [sb(f"par{i}", [P, X_END]) for i in range(PR)]
        bo_row = [sb(f"bo_row{i}", [P, D]) for i in range(PR)]
        zg = [sb(f"zg{i}", [P, SUBS, D]) for i in range(2)]
        xa = sb("xa", [P, TILE])
        xh = sb("xh", [P, DC, TILE], F32R)
        xl = sb("xl", [P, DC, TILE], F32R)
        gate_in = [sb(f"gate_in{i}", [P, TILE]) for i in range(2)]
        hid = [sb(f"hid{i}", [P, TILE]) for i in range(2)]
        HR = 3
        hh = [sb(f"hh{i}", [P, TILE], F32R) for i in range(HR)]
        hl = [sb(f"hl{i}", [P, TILE], F32R) for i in range(HR)]
        yo = [sb(f"yo{i}", [P, 2, D]) for i in range(2)]

        up_bank = [banks[0], banks[1]]
        gate_bank = [banks[3], banks[4]]
        down_bank = [banks[5], banks[6]]
        x_bank = [banks[2], banks[7]]

        src_of = (a["W1"].rearrange("e (c p) n -> e p c n", p=P),
                  a["W2"].rearrange("e (c p) n -> e p c n", p=P),
                  a["Wo"].rearrange("e (a m p) n -> e p a m n", a=2, p=P))
        expert_reg = {}

        def load_weights(j):
            if j == 0:
                sp.wait(t_tile_expert, *stage1_stores)
            for w in range(3):
                if j:
                    sp.wait(t["split", j - 1, w])
                fl = f_raw[w]
                fl.count += 16

                def issue(e, w=w, fl=fl):
                    if w == 0:
                        expert_reg[0] = e.value_load(tile_expert[0:1, j:j + 1], min_val=0,
                                                     max_val=EXPERTS - 1)
                    dst = raw[w][:, :, :]
                    src = src_of[w][bass.ds(expert_reg[0], 1)]
                    if w == 2:
                        dst = dst.rearrange("p a (m n) -> p a m n", n=D)
                        src = src.rearrange("e p a m n -> (e p) a m n")
                    else:
                        src = src.rearrange("e p c n -> (e p) c n")
                    return e.dma_start(dst, src).then_inc(fl.sem, 16)

                sp.do(issue)
                t["raw", j, w] = fl.token
            if j >= PR:
                sp.wait(t["tile_done", j - PR])
            fl = f_par[j % PR]
            fl.count += 32

            def issue_par(e, fl=fl):
                e.dma_start(par[j % PR][:, :], a["par"][bass.ds(expert_reg[0], 1)].rearrange(
                    "e p n -> (e p) n")).then_inc(fl.sem, 16)
                e.dma_start(bo_row[j % PR][:, :], a["bo"][bass.ds(expert_reg[0], 1), :]
                            .broadcast_to([P, D])).then_inc(fl.sem, 16)

            sp.do(issue_par)
            t["par", j] = fl.token

        def split_weights(j, w, c):
            q = j % 2
            act.wait(t["raw", j, w])
            if j >= 2:
                act.wait(t["down", j - 2, HC - 1])
            tok = act.sig(lambda e: e.activation(wh[q][:, w, c, :], raw[w][:, c, :], ACTF.Copy))
            dve.wait(tok)
            tok = dve.sig(lambda e: e.tensor_tensor(wl[q][:, w, c, :], raw[w][:, c, :],
                                                    wh[q][:, w, c, :].bitcast(F32),
                                                    ALU.subtract))
            t["split", j, w] = tok

        def gather(j):
            if j == 0:
                pool.wait(t_rows, f_dump.token, *stage1_stores)
            if j >= 2:
                pool.wait(t["x_t", j - 2])
            fl = f_gather[j % 2]
            for s in range(SUBS):
                fl.count += 16
                blk = j * SUBS + s
                pool.do(lambda e, s=s, blk=blk: e.indirect_dma_start(
                    out=zg[j % 2][:, s, :], out_offset=None, in_=z_rows,
                    in_offset=bass.IndirectOffsetOnAxis(ap=row_of[:, blk:blk + 1], axis=0))
                    .then_inc(fl.sem, 16))
            t["gather", j] = fl.token

        def expert_input(j):
            pe.wait(t["gather", j])
            dve.wait(t["par", j])
            for c in range(DC):
                if j:
                    pe.wait(t["x_free", j - 1, c])
                ps = x_bank[c]
                for s in range(SUBS):
                    tok = pe.sig(lambda e, c=c, s=s, ps=ps: e.transpose(
                        ps[:, s * P:(s + 1) * P], zg[j % 2][:, s, c * P:(c + 1) * P], ident))
                t["x_t", j] = tok
            for c in range(DC):
                ps = x_bank[c]
                dve.wait(t["x_t", j])
                if j or c:
                    dve.wait(t["xa_read"])
                tok = dve.sig(lambda e, c=c, ps=ps: e.tensor_scalar(
                    xa[:, :], ps[:, 0:TILE], par[j % PR][:, X_G + c:X_G + c + 1],
                    par[j % PR][:, X_B + c:X_B + c + 1], ALU.mult, ALU.add))
                t["x_free", j, c] = tok
                if j:
                    act.wait(t["up", j - 1, HC - 1])
                act.wait(tok)
                tok = act.sig(lambda e, c=c: e.activation(xh[:, c, :], xa[:, :], ACTF.Copy))
                dve.wait(tok)
                tok = dve.sig(lambda e, c=c: e.tensor_tensor(
                    xl[:, c, :], xa[:, :], xh[:, c, :].bitcast(F32), ALU.subtract))
                t["xa_read"] = tok
            t["x", "in", j] = tok

        def up(j, m):
            q, n = j % 2, (j * HC + m) % 2
            r = (j * HC + m) % HR
            before = t.get(("hidden", j * HC + m - 2))
            if m == 0:
                pe.wait(t["x", "in", j], *[t["split", j, w] for w in range(3)])
            for w, ps in ((1, gate_bank[n]), (0, up_bank[n])):
                if before:
                    pe.wait(before[w])
                products = [(wh, xh), (wh, xl), (wl, xh)]
                for c in range(DC):
                    for k, (ws, xx) in enumerate(products):
                        tok = pe.sig(lambda e, ws=ws, xx=xx, c=c, k=k, w=w, ps=ps: e.matmul(
                            ps[:, 0:TILE], ws[q][:, w, c, m * P:(m + 1) * P], xx[:, c, :],
                            start=(c == 0 and k == 0), stop=(c == DC - 1 and k == 2)))
                t["up" if w == 0 else "gate", j, m] = tok
            gi, h = gate_in[n], hid[n]
            p = par[j % PR]
            act.wait(t["gate", j, m], t["par", j])
            if before:
                act.wait(before[2])
            tok_g = act.sig(lambda e: e.activation(gi[:, :], gate_bank[n][:, 0:TILE],
                                                   ACTF.Identity,
                                                   bias=p[:, X_B2 + m:X_B2 + m + 1]))
            dve.wait(tok_g)
            tok = dve.sig(lambda e: e.tensor_scalar(gi[:, :], gi[:, :], CLIP_GATE, -CLIP_GATE,
                                                    ALU.min, ALU.max))
            act.wait(tok)
            tok = act.sig(lambda e: e.activation(gi[:, :], gi[:, :], ACTF.Silu))
            dve.wait(tok, t["up", j, m])
            if before:
                dve.wait(before[3])
            tok_u = dve.then(lambda e: e.scalar_tensor_tensor(
                h[:, :], up_bank[n][:, 0:TILE], p[:, X_B1 + m:X_B1 + m + 1], gi[:, :],
                ALU.add, ALU.mult))
            tok = dve.sig(lambda e: e.tensor_scalar(h[:, :], h[:, :], CLIP_OUT, -CLIP_OUT,
                                                    ALU.min, ALU.max))
            act.wait(tok)
            at = j * HC + m - HR
            if at >= 0:
                act.wait(t[("down",) + divmod(at, HC)])
            tok = act.sig(lambda e: e.activation(hh[r][:, :], h[:, :], ACTF.Copy))
            dve.wait(tok)
            tok = dve.sig(lambda e: e.tensor_tensor(hl[r][:, :], h[:, :],
                                                    hh[r][:, :].bitcast(F32), ALU.subtract))
            t["hidden", j * HC + m] = (tok_u, tok_g, tok_u, tok)

        def down(j, m):
            q, r = j % 2, (j * HC + m) % HR
            if m == 0 and j:
                pe.wait(*[t["down_free", j - 1, s] for s in range(-(-SUBS // 2))])
            pe.wait(t["hidden", j * HC + m][3])
            for s in range(SUBS):
                ps = down_bank[s // 2]
                w_of = lambda ws: ws[q][:, 2, m // 4, (m % 4) * D:(m % 4 + 1) * D]
                for k, (hs, ws) in enumerate(((hh, wh), (hh, wl), (hl, wh))):
                    tok = pe.sig(lambda e, s=s, k=k, hs=hs, w=w_of(ws), ps=ps: e.matmul(
                        ps[:, (s % 2) * D:(s % 2 + 1) * D], hs[r][:, s * P:(s + 1) * P], w,
                        start=(m == 0 and k == 0 and s % 2 == 0),
                        stop=(m == HC - 1 and k == 2), skip_group_check=True))
            t["down", j, m] = tok

        def finish_tile(j):
            q = j % 2
            for s2 in range(-(-SUBS // 2)):
                n = min(2, SUBS - 2 * s2)
                o = yo[s2][:, 0:n, :]
                dve.wait(t["down", j, HC - 1])
                if j:
                    dve.wait(t["scattered", j - 1])
                tok = dve.then(lambda e, s2=s2, n=n, o=o: e.tensor_tensor(
                    o, down_bank[s2][:, 0:n * D].rearrange("p (s d) -> p s d", d=D),
                    bo_row[j % PR][:, :].unsqueeze(1).broadcast_to([P, n, D]), ALU.add))
                t["down_free", j, s2] = tok
                t["tile_done", j] = tok
                tok = dve.sig(lambda e, o=o: e.tensor_scalar(o, o, CLIP_OUT, -CLIP_OUT, ALU.min,
                                                             ALU.max))
                act.wait(tok, t_gate)
                for s in range(n):
                    blk = j * SUBS + 2 * s2 + s
                    tok = act.sig(lambda e, s=s, s2=s2, blk=blk: e.activation(
                        yo[s2][:, s, :], yo[s2][:, s, :], ACTF.Copy,
                        scale=filled[:, 1, blk:blk + 1]))
                    pool.wait(tok)
                    if f_scatter.count:
                        pool.wait(f_scatter.token)
                    f_scatter.count += 16
                    pool.do(lambda e, s=s, s2=s2, blk=blk: e.indirect_dma_start(
                        out=out, out_offset=bass.IndirectOffsetOnAxis(
                            ap=row_of[:, blk:blk + 1], axis=0),
                        in_=yo[s2][:, s, :], in_offset=None, bounds_check=ROWS - 1,
                        oob_is_err=True, compute_op=ALU.add).then_inc(f_scatter.sem, 16))
            t["scattered", j] = f_scatter.token

        PIECES = [(1, 0), (1, 1), (0, 0), (0, 1), (2, 0), (2, 1)]
        load_weights(0)
        gather(0)
        for w, c in PIECES:
            split_weights(0, w, c)
        expert_input(0)
        LAG = 2
        for n in range(MAX_TILES * HC + LAG):
            j, m = divmod(n, HC)
            if j < MAX_TILES:
                up(j, m)
            if m == 0 and j + 1 < MAX_TILES:
                load_weights(j + 1)
                gather(j + 1)
            if j + 1 < MAX_TILES and 2 <= m:
                split_weights(j + 1, *PIECES[m - 2])
            if n >= LAG:
                jd, md = divmod(n - LAG, HC)
                down(jd, md)
                if md == HC - 1:
                    finish_tile(jd)
            if m == HC - 1 and j + 1 < MAX_TILES:
                expert_input(j + 1)
        pool.wait(f_scatter.token)

        block = ctx.enter_context(nc.Block())
        block.sync(lambda e: sp.emit(e))
        block.gpsimd(lambda e: pool.emit(e))
        block.scalar(lambda e: act.emit(e))
        block.vector(lambda e: dve.emit(e))
        block.tensor(lambda e: pe.emit(e))


def kernel(**inputs):
    import concourse.bacc as bacc
    from concourse.bass_utils import run_bass_kernel_spmd

    def columns(v):
        v = np.asarray(v)
        return v.reshape(-1, P).T

    def get(name):
        return np.asarray(inputs[name])

    wkv = get("L0_xattn_Wkv").reshape(D, HEADS, 2, HD)
    bkv = get("L0_xattn_bkv").reshape(HEADS, 2, HD)
    par = np.stack([np.concatenate([columns(get(n)[e]) for n in
                                    ("L0_ffn_eg", "L0_ffn_eb", "L0_ffn_b1", "L0_ffn_b2")], axis=1)
                    for e in range(EXPERTS)])
    arrays = {
        "x": get("x").reshape(TOKENS, D),
        "ctx": get("ctx_1024").reshape(BATCH * CTX, D),
        "wq": get("L0_xattn_Wq"),
        "wk": wkv[:, :, 0, :].reshape(D, D),
        "wv": wkv[:, :, 1, :].reshape(D, D),
        "wp": get("L0_xattn_Wp"),
        "qk_bias": np.concatenate([columns(get("L0_xattn_bq")),
                                   columns(bkv[:, 0, :].reshape(D))], axis=1),
        "bv": bkv[:, 1, :].reshape(1, D),
        "bp": get("L0_xattn_bp").reshape(1, D),
        "ln_g": get("L0_ffn_ln_g").reshape(1, D),
        "ln_b": get("L0_ffn_ln_b").reshape(1, D),
        "router": get("L0_ffn_router_w"),
        "W1": get("L0_ffn_W1"),
        "W2": get("L0_ffn_W2"),
        "Wo": get("L0_ffn_Wo"),
        "par": par,
        "bo": get("L0_ffn_bo"),
        "const": constants(),
    }
    nc = bacc.Bacc("TRN2", target_bir_lowering=False, num_devices=1)
    feed, aps = {}, {}
    for name, v in arrays.items():
        v = np.ascontiguousarray(v)
        feed[f"in_{name}"] = v
        aps[name] = nc.dram_tensor(f"in_{name}", v.shape, mybir.dt.from_np(v.dtype),
                                   kind="ExternalInput").ap()
    out = nc.dram_tensor("out_rows", [ROWS, D], F32, kind="ExternalOutput").ap()
    build(nc, aps, out)
    r = run_bass_kernel_spmd(nc, [feed], core_ids=[0])
    return r.results[0]["out_rows"][0:TOKENS].reshape(BATCH, SEQ, D)
```

```python
from contextlib import ExitStack

import numpy as np

import concourse.bass as bass
from concourse import mybir
from concourse.alu_op_type import AluOpType as ALU

F32 = mybir.dt.float32
F32R = mybir.dt.float32r
BF16 = mybir.dt.bfloat16
I32 = mybir.dt.int32
U32 = mybir.dt.uint32
ACTF = mybir.ActivationFunctionType
AXX = mybir.AxisListType.X

P = 128
BATCH, SEQ, D = 16, 256, 256
CTX = 77
HEADS, HD = 16, 16
EXPERTS, HIDDEN = 8, 1024
EPS = 1e-5
CLIP_OUT = 10000.0
CLIP_GATE = 20.0

TOKENS = BATCH * SEQ
NT = TOKENS // P
DC = D // P
HC = HIDDEN // P
HPC = HEADS // DC
KEYS = HEADS * CTX
KB = -(-KEYS // P)
TAIL = KEYS - (KB - 1) * P
BLOCK_HEADS = 3
VW = HD + 1

TILE = 512
SUBS = TILE // P
MAX_TILES = (2 * TOKENS + EXPERTS * (TILE - 1)) // TILE
SLOT_BLOCKS = MAX_TILES * SUBS
ROWS = TOKENS + P

C_IDENT = 0
C_TRI = C_IDENT + P
C_IOTA = C_TRI + P
C_KMASK = C_IOTA + P
C_VMASK = C_KMASK + HPC
C_TOKEN = C_VMASK + KB * BLOCK_HEADS
C_DUMP = C_TOKEN + NT
C_THR = C_DUMP + 1
NTHR = -(-TOKENS // TILE)
C_END = C_THR + NTHR

X_G, X_B, X_B1, X_B2 = 0, DC, 2 * DC, 2 * DC + HC
X_END = 2 * DC + 2 * HC


def block_heads(i):
    first = i * P // CTX
    last = min(i * P + P - 1, KEYS - 1) // CTX
    return first, last - first + 1


def constants():
    c = np.zeros((P, C_END), np.float32)
    p = np.arange(P)
    c[:, C_IDENT:C_IDENT + P] = np.eye(P)
    c[:, C_TRI:C_TRI + P] = p[:, None] < p[None, :]
    c[:, C_IOTA:C_IOTA + P] = p[None, :]
    c[:, C_KMASK:C_KMASK + HPC] = (p[:, None] // HD) == np.arange(HPC)[None, :]
    for i in range(KB):
        first, n = block_heads(i)
        for j in range(BLOCK_HEADS):
            c[:, C_VMASK + i * BLOCK_HEADS + j] = (i * P + p) // CTX == first + j
    c[:, C_TOKEN:C_TOKEN + NT] = 1 + p[:, None] + P * np.arange(NT)[None, :]
    c[:, C_DUMP] = TOKENS + 1 + p
    c[:, C_THR:C_THR + NTHR] = TILE * np.arange(NTHR)[None, :]
    return c


class Queue:

    def __init__(self, sem):
        self.sem, self.count, self.items, self.reached = sem, 0, [], {}

    def do(self, fn):
        self.items.append(fn)

    def sig(self, fn):
        self.count += 1
        self.items.append(lambda e: fn(e).then_inc(self.sem, 1))
        return self.sem, self.count

    def wait(self, *tokens):
        for sem, value in tokens:
            if self.reached.get(id(sem), 0) < value:
                self.reached[id(sem)] = value
                self.items.append(lambda e, sem=sem, value=value: e.wait_ge(sem, value))

    def then(self, fn):
        token = self.sig(fn)
        self.wait(token)
        return token

    def dma(self, flow, out, in_):
        flow.count += 16
        self.items.append(lambda e: e.dma_start(out, in_).then_inc(flow.sem, 16))
        return flow.sem, flow.count

    def emit(self, engine):
        for item in self.items:
            item(engine)


class Flow:

    def __init__(self, sem):
        self.sem, self.count = sem, 0

    @property
    def token(self):
        return self.sem, self.count


def build(nc, a, out):
    ctx = ExitStack()

    scope = [ctx]

    def sb(name, shape, dt=F32):
        return scope[-1].enter_context(nc.sbuf_tensor(name, shape, dt))

    def sem(name):
        return ctx.enter_context(nc.semaphore(name))

    def flow(name):
        return Flow(sem(name))

    PR = 4
    with ctx:
        z_rows = nc.dram_tensor("z_rows", [ROWS, D], F32, kind="Internal").ap()
        v_flat = nc.dram_tensor("v_flat", [BATCH, KEYS, VW], F32, kind="Internal").ap()

        pe, act, dve, pool, sp = (Queue(sem(n)) for n in
                                  ("pe_done", "act_done", "dve_done", "pool_done", "sp_done"))
        f_const, f_weights = flow("f_const"), flow("f_weights")
        f_x = [flow(f"f_x{i}") for i in range(8)]
        f_ctx = [flow(f"f_ctx{i}") for i in range(2)]
        f_vstore = [flow(f"f_vstore{i}") for i in range(2)]
        f_vload = [flow(f"f_vload{i}") for i in range(2)]
        f_x1 = [flow(f"f_x1_{i}") for i in range(3)]
        f_z = [flow(f"f_z{i}") for i in range(3)]
        f_dump = flow("f_dump")
        f_raw = [flow(f"f_raw{i}") for i in range(3)]
        f_par = [flow(f"f_par{i}") for i in range(PR)]
        f_gather = [flow(f"f_gather{i}") for i in range(2)]
        f_scatter = flow("f_scatter")

        banks = [ctx.enter_context(nc.psum_tensor(f"bank{i}", [P, 512], F32)) for i in range(8)]

        const = sb("const", [P, C_END])
        ident = const[:, C_IDENT:C_IDENT + P]
        half = sb("half", [P, 1])
        zeros = sb("zeros", [P, D])
        logits = sb("logits", [P, NT, EXPERTS])
        scope.append(ExitStack())
        wq, wk, wv, wp = (sb(n, [P, DC, D]) for n in ("wq", "wk", "wv", "wp"))
        router = sb("router", [P, DC, EXPERTS])
        qk_bias = sb("qk_bias", [P, 2 * DC])
        rows = sb("rows", [P, 4, D])
        bv_row, bp_row, g_row, b_row = (rows[:, i, :] for i in range(4))

        sp.dma(f_const, const[:, :], a["const"])
        sp.dma(f_const, qk_bias[:, :], a["qk_bias"])
        for i, n in enumerate(("bv", "bp", "ln_g", "ln_b")):
            sp.dma(f_const, rows[:, i, :], a[n].broadcast_to([P, D]))
        t_const = f_const.token


        XR, XBR, XFR = 8, 8, 4
        xs = [sb(f"xs{i}", [P, D]) for i in range(XR)]
        cs = [sb(f"cs{i}", [CTX, D]) for i in range(2)]
        c_t = sb("c_t", [P, DC, CTX])
        k_t = sb("k_t", [P, DC, CTX])
        k_blocks = [sb(f"k_blocks{i}", [P, DC, HPC, CTX]) for i in range(2)]
        v_sb = [sb(f"v_sb{i}", [CTX, HEADS, VW]) for i in range(2)]
        v_rep = [sb(f"v_rep{i}", [P, KB, VW]) for i in range(2)]
        v_blocks = [sb(f"v_blocks{i}", [P, KB, BLOCK_HEADS, VW]) for i in range(2)]
        xn = [sb(f"xn{i}", [P, D]) for i in range(2)]
        xn_t = [sb(f"xn_t{i}", [P, DC, SEQ]) for i in range(2)]
        q_t = [sb(f"q_t{i}", [P, DC, SEQ]) for i in range(2)]
        probs = [sb(f"probs{i}", [P, HEADS, CTX]) for i in range(2)]
        probs_t = [sb(f"probs_t{i}", [P, KB, P]) for i in range(2)]
        attn = [sb(f"attn{i}", [P, D]) for i in range(2)]
        attn_t = [sb(f"attn_t{i}", [P, DC, P]) for i in range(2)]
        xb = [sb(f"xb{i}", [P, D]) for i in range(XBR)]
        x1 = [sb(f"x1_{i}", [P, D]) for i in range(3)]
        y = [sb(f"y{i}", [P, D]) for i in range(2)]
        xf = [sb(f"xf{i}", [P, D]) for i in range(XFR)]
        xf_t = [sb(f"xf_t{i}", [P, DC, P]) for i in range(2)]
        z = [sb(f"z{i}", [P, D]) for i in range(3)]
        small = sb("small", [P, NT, 16])
        maxes = [sb(f"maxes{i}", [P, HEADS]) for i in range(2)]
        recip = [sb(f"recip{i}", [P, HEADS]) for i in range(2)]
        stats = sb("stats", [P, 3, NT, 6])

        score_bank = banks[0:3]
        trans_bank = banks[3:5]
        value_bank = banks[5]
        misc_bank = banks[6:8]
        score_free = [None] * 3
        trans_free = [None] * 2
        value_free = None
        misc_free = [None, None]
        turn = {"misc": 0, "score": 0, "trans": 0}

        def take(kind, free, queue):
            n = turn[kind] % len(free)
            turn[kind] += 1
            if free[n]:
                queue.wait(free[n])
            return n

        t = {}

        SCALE = 1.0 / float(np.sqrt(HD))
        bq_scaled = sb("bq_scaled", [P, DC])
        dve.wait(t_const)
        t_bq = dve.sig(lambda e: e.tensor_scalar(bq_scaled[:, :], qk_bias[:, 0:DC], SCALE, None,
                                                 ALU.mult))
        t_half = pool.sig(lambda e: e.memset(half[:, :], -0.5))
        t_zero = pool.sig(lambda e: e.memset(zeros[:, :], 0.0))
        t_ones = [pool.sig(lambda e, i=i: e.memset(v_sb[i][:, :, HD:VW], 1.0)) for i in range(2)]

        def load_x(i):
            if i >= XR:
                sp.wait(t["xb", i - XR], t["xn", i - XR])
            t["x", i] = sp.dma(f_x[i % XR], xs[i % XR][:, :], a["x"][i * P:(i + 1) * P, :])

        def load_ctx(b):
            if b >= 2:
                sp.wait(t["ctx_t", b - 2])
            t["ctx", b] = sp.dma(f_ctx[b % 2], cs[b % 2][:, :], a["ctx"][b * CTX:(b + 1) * CTX, :])

        def rsqrt_on_pool(dst, src):
            pool.then(lambda e: e.tensor_scalar(dst, src, EPS, None, ALU.add))
            return pool.then(lambda e: e.tensor_tensor(dst, dst, half[:, :], ALU.pow))

        def norm_stats(which, i, src):
            st = stats[:, which, i, :]
            mv = small[:, i, 4 * which:4 * which + 2]
            dve.then(lambda e: e.bn_stats(st, src))
            return dve.sig(lambda e: e.bn_aggr(mv, st))

        def keys_values(b):
            n = take("misc", misc_free, pe)
            pe.wait(t["ctx", b], t_const)
            ps = misc_bank[n]
            for c in range(DC):
                tok = pe.sig(lambda e, c=c: e.transpose(ps[:, c * CTX:(c + 1) * CTX],
                                                        cs[b % 2][:, c * P:(c + 1) * P],
                                                        ident[0:CTX, 0:CTX]))
            t["ctx_t", b] = tok
            act.wait(tok)
            if b:
                act.wait(t["kv_mm", b - 1])
            tok = act.sig(lambda e: e.activation(c_t[:, :, :], ps[:, 0:DC * CTX].rearrange(
                "p (c k) -> p c k", c=DC), ACTF.Copy))
            misc_free[n] = tok
            n = take("misc", misc_free, pe)
            pe.wait(tok, t_weights)
            psk = misc_bank[n]
            for m in range(DC):
                for c in range(DC):
                    tk = pe.sig(lambda e, m=m, c=c: e.matmul(
                        psk[:, m * CTX:(m + 1) * CTX], wk[:, c, m * P:(m + 1) * P], c_t[:, c, :],
                        start=(c == 0), stop=(c == DC - 1)))
            nv = take("misc", misc_free, pe)
            psv = misc_bank[nv]
            for c in range(DC):
                tv = pe.sig(lambda e, c=c: e.matmul(psv[0:CTX, 0:D], c_t[:, c, :], wv[:, c, :],
                                                    start=(c == 0), stop=(c == DC - 1)))
            t["kv_mm", b] = tv
            act.wait(tk, t_const)
            if b:
                act.wait(t["k_blocks", b - 1])
            for m in range(DC):
                tok = act.sig(lambda e, m=m: e.activation(
                    k_t[:, m, :], psk[:, m * CTX:(m + 1) * CTX], ACTF.Identity,
                    bias=qk_bias[:, DC + m:DC + m + 1]))
            misc_free[n] = tok
            pool.wait(tok)
            if b >= 2:
                pool.wait(t["scores", 2 * (b - 2) + 1])
            for m in range(DC):
                tok = pool.sig(lambda e, m=m: e.tensor_tensor(
                    k_blocks[b % 2][:, m, :, :],
                    k_t[:, m, :].unsqueeze(1).broadcast_to([P, HPC, CTX]),
                    const[:, C_KMASK:C_KMASK + HPC].unsqueeze(2).broadcast_to([P, HPC, CTX]),
                    ALU.mult))
            t["k_blocks", b] = tok
            dve.wait(tv, t_const, t_ones[1])
            if b >= 2:
                dve.wait(t["v_store", b - 2])
            tok = dve.sig(lambda e: e.tensor_tensor(
                v_sb[b % 2][:, :, 0:HD],
                psv[0:CTX, 0:D].rearrange("k (h d) -> k h d", h=HEADS),
                bv_row[0:CTX, :].rearrange("k (h d) -> k h d", h=HEADS), ALU.add))
            misc_free[nv] = tok
            sp.wait(tok)
            t["v_store", b] = sp.dma(f_vstore[b % 2],
                                     v_flat[b].rearrange("(h k) d -> k h d", h=HEADS),
                                     v_sb[b % 2][:, :, :])

        def load_values(b):
            sp.wait(t["v_store", b])
            if b >= 2:
                sp.wait(t["v_blocks", b - 2])
            full = (KB - 1) * P
            sp.dma(f_vload[b % 2], v_rep[b % 2][:, 0:KB - 1, :],
                   v_flat[b][0:full, :].rearrange("(i p) d -> p i d", p=P))
            t["v_load", b] = sp.dma(f_vload[b % 2], v_rep[b % 2][0:TAIL, KB - 1, :],
                                    v_flat[b][full:KEYS, :])

        def spread_values(b):
            pool.wait(t["v_load", b], t_const)
            if b >= 2:
                pool.wait(t["values", 2 * (b - 2) + 1])
            vm = const[:, C_VMASK:C_VMASK + KB * BLOCK_HEADS].rearrange(
                "p (i j) -> p i j", i=KB)
            for j in range(BLOCK_HEADS):
                for parts, lo, hi in ((P, 0, KB - 1), (TAIL, KB - 1, KB)):
                    tok = pool.sig(lambda e, j=j, parts=parts, lo=lo, hi=hi: e.tensor_tensor(
                        v_blocks[b % 2][0:parts, lo:hi, j, :], v_rep[b % 2][0:parts, lo:hi, :],
                        vm[0:parts, lo:hi, j:j + 1].broadcast_to([parts, hi - lo, VW]),
                        ALU.mult))
            t["v_blocks", b] = tok

        def x_stats(i):
            dve.wait(t["x", i])
            tok = norm_stats(0, i, xs[i % XR][:, :])
            pool.wait(tok, t_half)
            sm = small[:, i, :]
            t["x_stats", i] = rsqrt_on_pool(sm[:, 2:3], sm[:, 1:2])

        def x_norm(i):
            src, sm = xs[i % XR], small[:, i, :]
            dve.wait(t["x_stats", i])
            if i >= 2:
                dve.wait(t["xn_t", i - 2])
            t["xn", i] = dve.sig(lambda e: e.tensor_scalar(
                xn[i % 2][:, :], src[:, :], sm[:, 0:1], sm[:, 2:3], ALU.subtract, ALU.mult))
            pool.wait(t_const)
            if i >= XBR:
                pool.wait(t["x1", i - XBR])
            t["xb", i] = pool.sig(lambda e: e.tensor_tensor(
                xb[i % XBR][:, :], src[:, :], bp_row, ALU.add))

        def transpose_xn(i):
            b, s = divmod(i, 2)
            n = take("misc", misc_free, pe)
            ps = misc_bank[n]
            pe.wait(t["xn", i], t_const)
            for c in range(DC):
                tok = pe.sig(lambda e, c=c: e.transpose(
                    ps[:, c * P:(c + 1) * P], xn[i % 2][:, c * P:(c + 1) * P], ident))
            t["xn_t", i] = tok
            act.wait(tok)
            if b >= 2:
                act.wait(t["q_mm", b - 2])
            tok = act.sig(lambda e: e.activation(
                xn_t[b % 2][:, :, s * P:(s + 1) * P],
                ps[:, 0:DC * P].rearrange("p (c k) -> p c k", c=DC), ACTF.Copy))
            misc_free[n] = tok
            t["xn_t_sb", i] = tok

        def queries(b):
            n = take("misc", misc_free, pe)
            ps = misc_bank[n]
            pe.wait(t["xn_t_sb", 2 * b + 1], t_weights)
            for m in range(DC):
                for c in range(DC):
                    tok = pe.sig(lambda e, m=m, c=c: e.matmul(
                        ps[:, m * SEQ:(m + 1) * SEQ], wq[:, c, m * P:(m + 1) * P],
                        xn_t[b % 2][:, c, :], start=(c == 0), stop=(c == DC - 1)))
            t["q_mm", b] = tok
            act.wait(tok, t_bq)
            if b >= 2:
                act.wait(t["scores", 2 * (b - 2) + 1])
            for m in range(DC):
                tok = act.sig(lambda e, m=m: e.activation(
                    q_t[b % 2][:, m, :], ps[:, m * SEQ:(m + 1) * SEQ], ACTF.Identity,
                    bias=bq_scaled[:, m:m + 1], scale=SCALE))
            misc_free[n] = tok
            t["q", b] = tok

        HPB = HPC // 2

        def scores(i, u):
            b, s = divmod(i, 2)
            m, g = divmod(u, 2)
            n = take("score", score_free, pe)
            ps = score_bank[n]
            pe.wait(t["q", b], t["k_blocks", b])
            tok = pe.sig(lambda e: e.matmul(
                ps[:, 0:HPB * CTX], q_t[b % 2][:, m, s * P:(s + 1) * P],
                k_blocks[b % 2][:, m, g * HPB:(g + 1) * HPB, :].rearrange("p h k -> p (h k)"),
                start=True, stop=True))
            t["scores", i] = tok
            h0 = u * HPB
            view = ps[:, 0:HPB * CTX].rearrange("p (h k) -> p h k", h=HPB)
            mx = maxes[i % 2][:, h0:h0 + HPB]
            dve.wait(tok)
            if u == 0 and i >= 2:
                dve.wait(t["probs_t", i - 2])
            dve.then(lambda e: e.tensor_reduce(mx, view, AXX, ALU.max))
            tok = dve.sig(lambda e: e.tensor_tensor(
                probs[i % 2][:, h0:h0 + HPB, :], view,
                mx.unsqueeze(2).broadcast_to([P, HPB, CTX]), ALU.subtract))
            score_free[n] = tok
            if g == 1:
                act.wait(tok)
                part = probs[i % 2][:, m * HPC:(m + 1) * HPC, :]
                t["probs", i, m] = act.sig(lambda e: e.activation(part, part, ACTF.Exp))

        def transpose_probs(i, g):
            n = take("trans", trans_free, pe)
            ps = trans_bank[n]
            flat = probs[i % 2][:, :, :].rearrange("p h k -> p (h k)")
            blocks = list(range(4 * g, min(4 * g + 4, KB)))
            pe.wait(t["probs", i, 0 if (blocks[-1] + 1) * P <= HPC * CTX else 1])
            for j, k in enumerate(blocks):
                size = P if k < KB - 1 else TAIL
                tok = pe.sig(lambda e, j=j, k=k, size=size: e.transpose(
                    ps[0:size, j * P:(j + 1) * P], flat[:, k * P:k * P + size], ident))
            t["probs_t", i] = tok
            queue = (act, dve, act)[g]
            queue.wait(tok)
            if i >= 2:
                queue.wait(t["values", i - 2])
            whole = [k for k in blocks if k < KB - 1]
            pieces = [(P, 0, len(whole))] + ([(TAIL, len(whole), len(blocks))]
                                             if len(whole) < len(blocks) else [])
            for parts, lo, hi in pieces:
                dst = probs_t[i % 2][0:parts, blocks[0] + lo:blocks[0] + hi, :]
                src = ps[0:parts, lo * P:hi * P].rearrange("p (j k) -> p j k", k=P)
                if queue is act:
                    tok = act.sig(lambda e, dst=dst, src=src: e.activation(dst, src, ACTF.Copy))
                else:
                    tok = dve.sig(lambda e, dst=dst, src=src: e.tensor_copy(dst, src))
            trans_free[n] = tok
            t["probs_t_sb", i, g] = tok

        def values(i):
            nonlocal value_free
            b = i // 2
            if value_free:
                pe.wait(value_free)
            pe.wait(t["v_blocks", b])
            for k in range(KB):
                if k % 4 == 0:
                    pe.wait(t["probs_t_sb", i, k // 4])
                first, nh = block_heads(k)
                size = P if k < KB - 1 else TAIL
                tok = pe.sig(lambda e, k=k, first=first, nh=nh, size=size: e.matmul(
                    value_bank[:, first * VW:(first + nh) * VW],
                    probs_t[i % 2][0:size, k, :],
                    v_blocks[b % 2][0:size, k, 0:nh, :].rearrange("p j d -> p (j d)"),
                    start=(k == 0), stop=(k == KB - 1), skip_group_check=True))
            t["values", i] = tok
            dve.wait(tok)
            view = value_bank[:, 0:HEADS * VW].rearrange("p (h d) -> p h d", h=HEADS)
            dve.then(lambda e: e.reciprocal(recip[i % 2][:, :].unsqueeze(2), view[:, :, HD:VW]))
            if i >= 2:
                dve.wait(t["attn_t", i - 2])
            tok = dve.sig(lambda e: e.tensor_tensor(
                attn[i % 2][:, :].rearrange("p (h d) -> p h d", h=HEADS), view[:, :, 0:HD],
                recip[i % 2][:, :].unsqueeze(2).broadcast_to([P, HEADS, HD]), ALU.mult))
            value_free = tok
            t["attn", i] = tok

        def transposed_tile(i, src, src_token, dst, dst_readers, name):
            n = take("misc", misc_free, pe)
            ps = misc_bank[n]
            pe.wait(src_token)
            for c in range(DC):
                tok = pe.sig(lambda e, c=c: e.transpose(
                    ps[:, c * P:(c + 1) * P], src[:, c * P:(c + 1) * P], ident))
            t[name, i] = tok
            act.wait(tok, *dst_readers)
            tok = act.sig(lambda e: e.activation(
                dst[:, :, :], ps[:, 0:DC * P].rearrange("p (c k) -> p c k", c=DC), ACTF.Copy))
            misc_free[n] = tok
            return tok

        def transpose_attn(i):
            t["attn_t_sb", i] = transposed_tile(
                i, attn[i % 2], t["attn", i], attn_t[i % 2],
                [t["proj", i - 2]] if i >= 2 else [], "attn_t")

        def project(i):
            n = take("misc", misc_free, pe)
            ps = misc_bank[n]
            pe.wait(t["attn_t_sb", i], t_weights)
            for c in range(DC):
                tok = pe.sig(lambda e, c=c: e.matmul(ps[:, 0:D], attn_t[i % 2][:, c, :],
                                                     wp[:, c, :], start=(c == 0),
                                                     stop=(c == DC - 1)))
            t["proj", i] = tok
            dve.wait(tok, t["xb", i])
            if i >= 3:
                dve.wait(t["x1_store", i - 3])
            tok = dve.sig(lambda e: e.tensor_tensor(x1[i % 3][:, :], ps[:, 0:D], xb[i % XBR][:, :],
                                                    ALU.add))
            misc_free[n] = tok
            t["x1", i] = tok
            sp.wait(tok)
            t["x1_store", i] = sp.dma(f_x1[i % 3], out[i * P:(i + 1) * P, :], x1[i % 3][:, :])

            dve.wait(tok)
            tok = norm_stats(1, i, x1[i % 3][:, :])
            pool.wait(tok)
            sm = small[:, i, :]
            r1, r2 = sm[:, 12:13], sm[:, 13:14]
            rsqrt_on_pool(r1, sm[:, 5:6])
            pool.then(lambda e: e.tensor_tensor(r2, r1, r1, ALU.mult))
            pool.then(lambda e: e.tensor_tensor(r2, r2, sm[:, 5:6], ALU.mult))
            rsqrt_on_pool(r2, r2)
            t["x1_stats", i] = pool.sig(lambda e: e.tensor_tensor(sm[:, 6:7], r1, r2, ALU.mult))

        def x1_norm(i):
            sm = small[:, i, :]
            dve.wait(t["x1_stats", i])
            if i >= 2:
                dve.wait(t["xf", i - 2])
            tok = dve.sig(lambda e: e.tensor_scalar(y[i % 2][:, :], x1[i % 3][:, :], sm[:, 4:5],
                                                    sm[:, 6:7], ALU.subtract, ALU.mult))
            pool.wait(tok)
            if i >= XFR:
                pool.wait(t["xf_t", i - XFR], t["z", i - XFR])
            pool.then(lambda e: e.tensor_tensor(xf[i % XFR][:, :], y[i % 2][:, :], g_row,
                                                ALU.mult))
            t["xf", i] = pool.sig(lambda e: e.tensor_tensor(xf[i % XFR][:, :],
                                                            xf[i % XFR][:, :], b_row, ALU.add))

        def xf_stats(i):
            dve.wait(t["xf", i])
            tok = norm_stats(2, i, xf[i % XFR][:, :])
            sm = small[:, i, :]
            pool.wait(tok)
            t["xf_stats", i] = rsqrt_on_pool(sm[:, 10:11], sm[:, 9:10])

        def finish_norm(i):
            sm = small[:, i, :]
            dve.wait(t["xf_stats", i])
            if i >= 3:
                dve.wait(t["z_store", i - 3])
            tok = dve.sig(lambda e: e.tensor_scalar(z[i % 3][:, :], xf[i % XFR][:, :], sm[:, 8:9],
                                                    sm[:, 10:11], ALU.subtract, ALU.mult))
            t["z", i] = tok
            sp.wait(tok)
            t["z_store", i] = sp.dma(f_z[i % 3], z_rows[i * P:(i + 1) * P, :], z[i % 3][:, :])

        def transpose_xf(i):
            t["xf_t_sb", i] = transposed_tile(
                i, xf[i % XFR], t["xf", i], xf_t[i % 2],
                [t["logits_mm", i - 2]] if i >= 2 else [], "xf_t")

        def route_logits(i):
            n = take("misc", misc_free, pe)
            ps = misc_bank[n]
            pe.wait(t["xf_t_sb", i], t_weights)
            for c in range(DC):
                tok = pe.sig(lambda e, c=c: e.matmul(ps[:, 0:EXPERTS], xf_t[i % 2][:, c, :],
                                                     router[:, c, :], start=(c == 0),
                                                     stop=(c == DC - 1)))
            t["logits_mm", i] = tok
            act.wait(tok)
            tok = act.sig(lambda e: e.activation(logits[:, i, :], ps[:, 0:EXPERTS], ACTF.Copy))
            misc_free[n] = tok
            t["logits", i] = tok

        for i in range(XR):
            load_x(i)
        load_ctx(0)
        for dst, n in ((wk, "wk"), (wv, "wv"), (wq, "wq"), (wp, "wp"), (router, "router")):
            sp.dma(f_weights, dst[:, :, :], a[n].rearrange("(c p) n -> p c n", p=P))
        t_weights = f_weights.token
        load_ctx(1)
        sp.wait(t_zero)
        sp.dma(f_dump, z_rows[TOKENS:ROWS, :], zeros[:, :])
        sp.dma(f_dump, out[TOKENS:ROWS, :], zeros[:, :])

        def step(fn, tile, *more):
            if 0 <= tile < NT:
                fn(tile, *more)

        for i in range(-5, NT + 5):
            even = i % 2 == 0
            nb = i // 2 + 1
            if i + 7 >= XR:
                step(load_x, i + 7)
            step(scores, i, 0)
            step(scores, i, 1)
            step(transpose_probs, i - 1, 0)
            step(scores, i, 2)
            step(transpose_attn, i - 2)
            step(transpose_probs, i - 1, 1)
            step(scores, i, 3)
            step(x1_norm, i - 3)
            step(transpose_probs, i - 1, 2)
            step(project, i - 2)
            if not even and 0 <= nb < BATCH:
                queries(nb)
            step(xf_stats, i - 4)
            step(finish_norm, i - 5)
            step(x_stats, i + 5)
            step(transpose_xn, i + 3)
            step(x_norm, i + 4)
            step(values, i - 1)
            if even and 0 <= nb < BATCH:
                keys_values(nb)
                if nb + 2 < BATCH:
                    load_ctx(nb + 2)
            step(transpose_xf, i - 4)
            if not even and 0 <= nb < BATCH:
                load_values(nb)
                spread_values(nb)
            step(route_logits, i - 5)

        scope.pop().close()
        stage1_stores = [t[n, i] for n in ("x1_store", "z_store") for i in range(NT - 3, NT)]

        best = sb("best", [P, NT, 8])
        best_idx = sb("best_idx", [P, NT, 8], U32)
        pick = sb("pick", [P, 2, NT])
        gates = sb("gates", [P, 2, NT])
        gate_sum = sb("gate_sum", [P, NT])
        chosen = sb("chosen", [P, 2, NT, EXPERTS])
        both = sb("both", [P, NT, EXPERTS], BF16)
        tri = sb("tri", [P, P], BF16)
        ones = sb("ones", [P, P], BF16)
        totals = sb("totals", [P, NT, EXPERTS])
        running = sb("running", [P, EXPERTS, NT])
        zero8 = sb("zero8", [P, NT])
        place = sb("place", [P, NT, EXPERTS])
        over = sb("over", [P, EXPERTS, NTHR])
        n_tiles = sb("n_tiles", [P, EXPERTS])
        tile_end = sb("tile_end", [P, EXPERTS])
        tile_start = sb("tile_start", [P, EXPERTS])
        base = sb("base", [P, EXPERTS])
        begun = sb("begun", [1, MAX_TILES, EXPERTS])
        tile_expert_f = sb("tile_expert_f", [1, MAX_TILES])
        tile_expert = sb("tile_expert", [1, MAX_TILES], I32)
        slot = sb("slot", [P, 2, NT])
        slot_i = sb("slot_i", [P, 2, NT], I32)
        hi_lo_i = sb("hi_lo_i", [P, 2, 2, NT], I32)
        hi_lo = sb("hi_lo", [P, 2, 2, NT])
        AR = 4
        at_lo = [sb(f"at_lo{i}", [P, P]) for i in range(AR)]
        at_hi = [sb(f"at_hi{i}", [P, 2, SLOT_BLOCKS]) for i in range(AR)]
        filled = sb("filled", [P, 2, SLOT_BLOCKS])
        dump = sb("dump", [P, SLOT_BLOCKS])
        row_of = sb("row_of", [P, SLOT_BLOCKS], I32)

        iota = const[:, C_IOTA:C_IOTA + P]
        dve.wait(t_const)
        dve.sig(lambda e: e.tensor_copy(tri[:, :], const[:, C_TRI:C_TRI + P]))
        dve.sig(lambda e: e.memset(ones[:, :], 1.0))
        dve.sig(lambda e: e.memset(zero8[:, :], 0.0))
        dve.wait(t["logits", NT - 1])
        for i in range(NT):
            tok = dve.sig(lambda e, i=i: e.max(best[:, i, :], logits[:, i, :]))
        dve.wait(tok)
        for i in range(NT):
            tok = dve.sig(lambda e, i=i: e.max_index(best_idx[:, i, :], best[:, i, :],
                                                     logits[:, i, :]))
        tok2 = dve.then(lambda e: e.tensor_tensor(gates[:, 1, :], best[:, :, 1], best[:, :, 0],
                                                  ALU.subtract))
        act.wait(tok2)
        tok2 = act.sig(lambda e: e.activation(gates[:, 1, :], gates[:, 1, :], ACTF.Exp))
        dve.then(lambda e: e.tensor_copy(pick[:, :, :], best_idx[:, :, 0:2].rearrange(
            "p t k -> p k t")))
        for k in range(2):
            tok = dve.sig(lambda e, k=k: e.tensor_tensor(
                chosen[:, k, :, :], pick[:, k, :].unsqueeze(2).broadcast_to([P, NT, EXPERTS]),
                iota[:, 0:EXPERTS].unsqueeze(1).broadcast_to([P, NT, EXPERTS]), ALU.is_equal))
        dve.wait(tok)
        tok = dve.sig(lambda e: e.tensor_tensor(both[:, :, :], chosen[:, 0, :, :],
                                                chosen[:, 1, :, :], ALU.add))
        pe.wait(tok)
        pe.wait(*[f for f in score_free if f])
        flat_both = both[:, :, :].rearrange("p t e -> p (t e)")
        nte = NT * EXPERTS
        tok_pre = pe.sig(lambda e: e.matmul(banks[0][:, 0:nte], tri[:, :], flat_both, start=True,
                                            stop=True))
        tok_tot = pe.sig(lambda e: e.matmul(banks[1][:, 0:nte], ones[:, :], flat_both, start=True,
                                            stop=True))
        dve.wait(tok2)
        dve.then(lambda e: e.tensor_scalar(gate_sum[:, :], gates[:, 1, :], 1.0, None, ALU.add))
        dve.then(lambda e: e.reciprocal(gates[:, 0, :], gate_sum[:, :]))
        dve.then(lambda e: e.tensor_tensor(gates[:, 1, :], gates[:, 1, :], gates[:, 0, :],
                                           ALU.mult))
        dve.wait(tok_tot)
        dve.then(lambda e: e.tensor_copy(totals[:, :, :], banks[1][:, 0:nte].rearrange(
            "p (t e) -> p t e", t=NT)))
        for x in range(EXPERTS):
            tok = dve.sig(lambda e, x=x: e.tensor_tensor_scan(
                running[:, x, :], totals[:, :, x], zero8[:, :], 0.0, ALU.add, ALU.add))
        dve.wait(tok)
        dve.then(lambda e: e.tensor_tensor(
            over[:, :, :], running[:, :, NT - 1:NT].broadcast_to([P, EXPERTS, NTHR]),
            const[:, C_THR:C_THR + NTHR].unsqueeze(1).broadcast_to([P, EXPERTS, NTHR]),
            ALU.is_gt))
        dve.then(lambda e: e.tensor_reduce(n_tiles[:, :], over[:, :, :], AXX, ALU.add))
        dve.then(lambda e: e.tensor_tensor_scan(tile_end[:, :], n_tiles[:, :],
                                                zero8[:, 0:EXPERTS], 0.0, ALU.add, ALU.add))
        dve.then(lambda e: e.tensor_tensor(tile_start[:, :], tile_end[:, :], n_tiles[:, :],
                                           ALU.subtract))
        dve.then(lambda e: e.tensor_scalar(base[:, :], tile_start[:, :], float(TILE), None,
                                           ALU.mult))
        dve.then(lambda e: e.tensor_tensor(
            begun[:, :, :],
            tile_start[0:1, :].unsqueeze(1).broadcast_to([1, MAX_TILES, EXPERTS]),
            iota[0:1, 0:MAX_TILES].unsqueeze(2).broadcast_to([1, MAX_TILES, EXPERTS]),
            ALU.is_le))
        dve.then(lambda e: e.tensor_reduce(tile_expert_f[:, :], begun[:, :, :], AXX, ALU.add))
        t_tile_expert = dve.sig(lambda e: e.tensor_scalar(
            tile_expert[:, :], tile_expert_f[:, :], -1.0, None, ALU.add))
        dve.wait(tok_pre)
        dve.then(lambda e: e.tensor_tensor(
            place[:, :, :], banks[0][:, 0:nte].rearrange("p (t e) -> p t e", t=NT),
            running[:, :, :].rearrange("p e t -> p t e"), ALU.add))
        dve.then(lambda e: e.tensor_tensor(place[:, :, :], place[:, :, :], totals[:, :, :],
                                           ALU.subtract))
        dve.then(lambda e: e.tensor_tensor(
            place[:, :, :], place[:, :, :],
            base[:, :].unsqueeze(1).broadcast_to([P, NT, EXPERTS]), ALU.add))
        for k in range(2):
            dve.then(lambda e, k=k: e.tensor_tensor(chosen[:, k, :, :], chosen[:, k, :, :],
                                                    place[:, :, :], ALU.mult))
            tok = dve.sig(lambda e, k=k: e.tensor_reduce(slot[:, k, :], chosen[:, k, :, :], AXX,
                                                         ALU.add))
        dve.wait(tok)
        dve.then(lambda e: e.tensor_copy(slot_i[:, :, :], slot[:, :, :]))
        dve.sig(lambda e: e.tensor_single_scalar(hi_lo_i[:, 0, :, :], slot_i[:, :, :], 7,
                                                 ALU.logical_shift_right))
        dve.then(lambda e: e.tensor_single_scalar(hi_lo_i[:, 1, :, :], slot_i[:, :, :], P - 1,
                                                  ALU.bitwise_and))
        dve.then(lambda e: e.tensor_copy(hi_lo[:, :, :, :], hi_lo_i[:, :, :, :]))
        fill_bank = banks[2]
        used = []
        for n in range(2 * NT):
            k, i = divmod(n, NT)
            if n >= AR:
                dve.wait(used[n - AR])
            lo, hi = hi_lo[:, 1, k, i:i + 1], hi_lo[:, 0, k, i:i + 1]
            dve.sig(lambda e, n=n, lo=lo: e.tensor_scalar(at_lo[n % AR][:, :], iota, lo, None,
                                                          ALU.is_equal))
            for w, value in enumerate((const[:, C_TOKEN + i:C_TOKEN + i + 1],
                                       gates[:, k, i:i + 1])):
                tok = dve.sig(lambda e, n=n, hi=hi, w=w, value=value: e.tensor_scalar(
                    at_hi[n % AR][:, w, :], iota[:, 0:SLOT_BLOCKS], hi, value, ALU.is_equal,
                    ALU.mult))
            pe.wait(tok)
            used.append(pe.sig(lambda e, n=n: e.matmul(
                fill_bank[:, 0:2 * SLOT_BLOCKS], at_lo[n % AR][:, :],
                at_hi[n % AR][:, :, :].rearrange("p w s -> p (w s)"), start=(n == 0),
                stop=(n == 2 * NT - 1))))
        dve.wait(used[-1])
        t_gate = dve.then(lambda e: e.tensor_copy(filled[:, :, :], fill_bank[
            :, 0:2 * SLOT_BLOCKS].rearrange("p (w s) -> p w s", w=2)))
        dve.then(lambda e: e.tensor_scalar(dump[:, :], filled[:, 0, :], 0.0,
                                           const[:, C_DUMP:C_DUMP + 1], ALU.is_equal, ALU.mult))
        t_rows = dve.sig(lambda e: e.scalar_tensor_tensor(
            row_of[:, :], filled[:, 0, :], -1.0, dump[:, :], ALU.add, ALU.add))

        raw = [sb(f"raw{i}", [P, 2, HIDDEN]) for i in range(3)]
        wh = [sb(f"wh{i}", [P, 3, 2, HIDDEN], F32R) for i in range(2)]
        wl = [sb(f"wl{i}", [P, 3, 2, HIDDEN], F32R) for i in range(2)]
        par = [sb(f"par{i}", [P, X_END]) for i in range(PR)]
        bo_row = [sb(f"bo_row{i}", [P, D]) for i in range(PR)]
        zg = [sb(f"zg{i}", [P, SUBS, D]) for i in range(2)]
        xa = sb("xa", [P, TILE])
        xh = [sb(f"xh{i}", [P, DC, TILE], F32R) for i in range(2)]
        xl = [sb(f"xl{i}", [P, DC, TILE], F32R) for i in range(2)]
        gate_in = [sb(f"gate_in{i}", [P, TILE]) for i in range(2)]
        hid = [sb(f"hid{i}", [P, TILE]) for i in range(2)]
        HR = 4
        hh = [sb(f"hh{i}", [P, TILE], F32R) for i in range(HR)]
        hl = [sb(f"hl{i}", [P, TILE], F32R) for i in range(HR)]
        yo = [sb(f"yo{i}", [P, 2, D]) for i in range(2)]

        up_bank = [banks[0], banks[1]]
        gate_bank = [banks[3], banks[4]]
        down_bank = [banks[5], banks[6]]
        x_bank = [banks[2], banks[7]]

        src_of = (a["W1"].rearrange("e (c p) n -> e p c n", p=P),
                  a["W2"].rearrange("e (c p) n -> e p c n", p=P),
                  a["Wo"].rearrange("e (a m p) n -> e p a m n", a=2, p=P))
        expert_reg = {}

        def load_expert(j):
            if j == 0:
                sp.wait(t_tile_expert, *stage1_stores)
            if j >= PR:
                sp.wait(t["tile_done", j - PR])
            fl = f_par[j % PR]
            fl.count += 32

            def issue(e):
                expert_reg[j] = e.value_load(tile_expert[0:1, j:j + 1], min_val=0,
                                             max_val=EXPERTS - 1)
                e.dma_start(par[j % PR][:, :], a["par"][bass.ds(expert_reg[j], 1)].rearrange(
                    "e p n -> (e p) n")).then_inc(fl.sem, 16)
                e.dma_start(bo_row[j % PR][:, :], a["bo"][bass.ds(expert_reg[j], 1), :]
                            .broadcast_to([P, D])).then_inc(fl.sem, 16)

            sp.do(issue)
            t["par", j] = fl.token

        def load_matrix(j, w):
            if j:
                sp.wait(t["split", j - 1, w])
            fl = f_raw[w]
            fl.count += 16

            def issue(e):
                src = src_of[w][bass.ds(expert_reg[j], 1)]
                if w == 2:
                    dst = raw[w][:, :, :].rearrange("p a (m n) -> p a m n", n=D)
                    src = src.rearrange("e p a m n -> (e p) a m n")
                else:
                    dst = raw[w][:, :, :]
                    src = src.rearrange("e p c n -> (e p) c n")
                return e.dma_start(dst, src).then_inc(fl.sem, 16)

            sp.do(issue)
            t["raw", j, w] = fl.token

        def split_weights(j, w, c):
            q = j % 2
            act.wait(t["raw", j, w])
            if j >= 2:
                act.wait(t["down" if w == 2 else "up", j - 2, HC - 1])
            tok = act.sig(lambda e: e.activation(wh[q][:, w, c, :], raw[w][:, c, :], ACTF.Copy))
            dve.wait(tok)
            tok = dve.sig(lambda e: e.tensor_tensor(wl[q][:, w, c, :], raw[w][:, c, :],
                                                    wh[q][:, w, c, :].bitcast(F32),
                                                    ALU.subtract))
            t["split", j, w] = tok

        def gather(j):
            if j == 0:
                pool.wait(t_rows, f_dump.token, *stage1_stores)
            if j >= 2:
                pool.wait(t["x_t", j - 2])
            fl = f_gather[j % 2]
            for s in range(SUBS):
                fl.count += 16
                blk = j * SUBS + s
                pool.do(lambda e, s=s, blk=blk: e.indirect_dma_start(
                    out=zg[j % 2][:, s, :], out_offset=None, in_=z_rows,
                    in_offset=bass.IndirectOffsetOnAxis(ap=row_of[:, blk:blk + 1], axis=0))
                    .then_inc(fl.sem, 16))
            t["gather", j] = fl.token

        def expert_input(j):
            pe.wait(t["gather", j])
            dve.wait(t["par", j])
            for c in range(DC):
                if j:
                    pe.wait(t["x_free", j - 1, c])
                ps = x_bank[c]
                for s in range(SUBS):
                    tok = pe.sig(lambda e, c=c, s=s, ps=ps: e.transpose(
                        ps[:, s * P:(s + 1) * P], zg[j % 2][:, s, c * P:(c + 1) * P], ident))
                t["x_t", j] = tok
            for c in range(DC):
                ps = x_bank[c]
                dve.wait(t["x_t", j])
                if j or c:
                    dve.wait(t["xa_read"])
                tok = dve.sig(lambda e, c=c, ps=ps: e.tensor_scalar(
                    xa[:, :], ps[:, 0:TILE], par[j % PR][:, X_G + c:X_G + c + 1],
                    par[j % PR][:, X_B + c:X_B + c + 1], ALU.mult, ALU.add))
                t["x_free", j, c] = tok
                if j >= 2:
                    act.wait(t["up", j - 2, HC - 1])
                act.wait(tok)
                tok = act.sig(lambda e, c=c: e.activation(xh[j % 2][:, c, :], xa[:, :], ACTF.Copy))
                dve.wait(tok)
                tok = dve.sig(lambda e, c=c: e.tensor_tensor(
                    xl[j % 2][:, c, :], xa[:, :], xh[j % 2][:, c, :].bitcast(F32), ALU.subtract))
                t["xa_read"] = tok
            t["x", "in", j] = tok

        def up(j, m):
            q, n = j % 2, (j * HC + m) % 2
            if m == 0:
                pe.wait(t["x", "in", j])
            for w, ps, reader in ((1, gate_bank[n], "gate_free"), (0, up_bank[n], "gated")):
                if m == 0:
                    pe.wait(t["split", j, w])
                if (reader, j * HC + m - 2) in t:
                    pe.wait(t[reader, j * HC + m - 2])
                products = [(wh, xh[q]), (wh, xl[q]), (wl, xh[q])]
                for c in range(DC):
                    for k, (ws, xx) in enumerate(products):
                        tok = pe.sig(lambda e, ws=ws, xx=xx, c=c, k=k, w=w, ps=ps: e.matmul(
                            ps[:, 0:TILE], ws[q][:, w, c, m * P:(m + 1) * P], xx[:, c, :],
                            start=(c == 0 and k == 0), stop=(c == DC - 1 and k == 2)))
                t["up" if w == 0 else "gate", j, m] = tok

        def gate_to_sbuf(j, m):
            n = (j * HC + m) % 2
            gi, bias = gate_in[n], par[j % PR][:, X_B2 + m:X_B2 + m + 1]
            act.wait(t["gate", j, m], t["par", j])
            if ("gated", j * HC + m - 2) in t:
                act.wait(t["gated", j * HC + m - 2])
            tok = act.sig(lambda e: e.activation(gi[:, :], gate_bank[n][:, 0:TILE],
                                                 ACTF.Identity, bias=bias))
            t["gate_free", j * HC + m] = tok
            dve.wait(tok)
            t["clipped", j, m] = dve.sig(lambda e: e.tensor_scalar(
                gi[:, :], gi[:, :], CLIP_GATE, -CLIP_GATE, ALU.min, ALU.max))

        def gated(j, m):
            n = (j * HC + m) % 2
            gi, h, bias = gate_in[n], hid[n], par[j % PR][:, X_B1 + m:X_B1 + m + 1]
            act.wait(t["clipped", j, m])
            tok = act.sig(lambda e: e.activation(gi[:, :], gi[:, :], ACTF.Silu))
            dve.wait(tok, t["up", j, m])
            t["gated", j * HC + m] = dve.then(lambda e: e.scalar_tensor_tensor(
                h[:, :], up_bank[n][:, 0:TILE], bias, gi[:, :], ALU.add, ALU.mult))
            t["hid", j, m] = dve.sig(lambda e: e.tensor_scalar(
                h[:, :], h[:, :], CLIP_OUT, -CLIP_OUT, ALU.min, ALU.max))

        def split_hidden(j, m):
            n, r = (j * HC + m) % 2, (j * HC + m) % HR
            at = j * HC + m - HR
            act.wait(t["hid", j, m])
            if at >= 0:
                act.wait(t[("down",) + divmod(at, HC)])
            tok = act.sig(lambda e: e.activation(hh[r][:, :], hid[n][:, :], ACTF.Copy))
            dve.wait(tok)
            t["hidden", j, m] = dve.sig(lambda e: e.tensor_tensor(
                hl[r][:, :], hid[n][:, :], hh[r][:, :].bitcast(F32), ALU.subtract))

        def down(j, m):
            q, r = j % 2, (j * HC + m) % HR
            if m == 0 and j:
                pe.wait(*[t["down_free", j - 1, s] for s in range(-(-SUBS // 2))])
            if m == 0:
                pe.wait(t["split", j, 2])
            pe.wait(t["hidden", j, m])
            for s in range(SUBS):
                ps = down_bank[s // 2]
                w_of = lambda ws: ws[q][:, 2, m // 4, (m % 4) * D:(m % 4 + 1) * D]
                for k, (hs, ws) in enumerate(((hh, wh), (hh, wl), (hl, wh))):
                    tok = pe.sig(lambda e, s=s, k=k, hs=hs, w=w_of(ws), ps=ps: e.matmul(
                        ps[:, (s % 2) * D:(s % 2 + 1) * D], hs[r][:, s * P:(s + 1) * P], w,
                        start=(m == 0 and k == 0 and s % 2 == 0),
                        stop=(m == HC - 1 and k == 2), skip_group_check=True))
            t["down", j, m] = tok

        def finish_tile(j):
            q = j % 2
            for s2 in range(-(-SUBS // 2)):
                n = min(2, SUBS - 2 * s2)
                o = yo[s2][:, 0:n, :]
                dve.wait(t["down", j, HC - 1])
                if j:
                    dve.wait(t["scattered", j - 1])
                tok = dve.then(lambda e, s2=s2, n=n, o=o: e.tensor_tensor(
                    o, down_bank[s2][:, 0:n * D].rearrange("p (s d) -> p s d", d=D),
                    bo_row[j % PR][:, :].unsqueeze(1).broadcast_to([P, n, D]), ALU.add))
                t["down_free", j, s2] = tok
                t["tile_done", j] = tok
                tok = dve.sig(lambda e, o=o: e.tensor_scalar(o, o, CLIP_OUT, -CLIP_OUT, ALU.min,
                                                             ALU.max))
                act.wait(tok, t_gate)
                for s in range(n):
                    blk = j * SUBS + 2 * s2 + s
                    tok = act.sig(lambda e, s=s, s2=s2, blk=blk: e.activation(
                        yo[s2][:, s, :], yo[s2][:, s, :], ACTF.Copy,
                        scale=filled[:, 1, blk:blk + 1]))
                    pool.wait(tok)
                    if f_scatter.count:
                        pool.wait(f_scatter.token)
                    f_scatter.count += 16
                    pool.do(lambda e, s=s, s2=s2, blk=blk: e.indirect_dma_start(
                        out=out, out_offset=bass.IndirectOffsetOnAxis(
                            ap=row_of[:, blk:blk + 1], axis=0),
                        in_=yo[s2][:, s, :], in_offset=None, bounds_check=ROWS - 1,
                        oob_is_err=True, compute_op=ALU.add).then_inc(f_scatter.sem, 16))
            t["scattered", j] = f_scatter.token

        PIECES = {1: (1, 0), 2: (1, 1), 3: (0, 0), 4: (0, 1), 6: (2, 0), 7: (2, 1)}
        load_expert(0)
        for w in (1, 0, 2):
            load_matrix(0, w)
        gather(0)
        for w, c in PIECES.values():
            split_weights(0, w, c)
        load_expert(1)
        for w in (1, 0, 2):
            load_matrix(1, w)
        expert_input(0)
        LAG = 3
        for n in range(MAX_TILES * HC + LAG):
            j, m = divmod(n, HC)
            if m == 0 and j + 1 < MAX_TILES:
                gather(j + 1)
            if m == 0 and j + 2 < MAX_TILES:
                load_expert(j + 2)
            if j < MAX_TILES:
                up(j, m)
                gate_to_sbuf(j, m)
            if 1 <= n <= MAX_TILES * HC:
                split_hidden(*divmod(n - 1, HC))
            if j + 1 < MAX_TILES and m in PIECES:
                w, c = PIECES[m]
                split_weights(j + 1, w, c)
                if c == 1 and j + 2 < MAX_TILES:
                    load_matrix(j + 2, w)
            if j < MAX_TILES:
                gated(j, m)
            if n >= LAG:
                jd, md = divmod(n - LAG, HC)
                down(jd, md)
                if md == HC - 1:
                    finish_tile(jd)
            if m == 5 and j + 1 < MAX_TILES:
                expert_input(j + 1)
        pool.wait(f_scatter.token)

        block = ctx.enter_context(nc.Block())
        block.sync(lambda e: sp.emit(e))
        block.gpsimd(lambda e: pool.emit(e))
        block.scalar(lambda e: act.emit(e))
        block.vector(lambda e: dve.emit(e))
        block.tensor(lambda e: pe.emit(e))


def kernel(**inputs):
    import concourse.bacc as bacc
    from concourse.bass_utils import run_bass_kernel_spmd

    def columns(v):
        v = np.asarray(v)
        return v.reshape(-1, P).T

    def get(name):
        return np.asarray(inputs[name])

    wkv = get("L0_xattn_Wkv").reshape(D, HEADS, 2, HD)
    bkv = get("L0_xattn_bkv").reshape(HEADS, 2, HD)
    par = np.stack([np.concatenate([columns(get(n)[e]) for n in
                                    ("L0_ffn_eg", "L0_ffn_eb", "L0_ffn_b1", "L0_ffn_b2")], axis=1)
                    for e in range(EXPERTS)])
    arrays = {
        "x": get("x").reshape(TOKENS, D),
        "ctx": get("ctx_1024").reshape(BATCH * CTX, D),
        "wq": get("L0_xattn_Wq"),
        "wk": wkv[:, :, 0, :].reshape(D, D),
        "wv": wkv[:, :, 1, :].reshape(D, D),
        "wp": get("L0_xattn_Wp"),
        "qk_bias": np.concatenate([columns(get("L0_xattn_bq")),
                                   columns(bkv[:, 0, :].reshape(D))], axis=1),
        "bv": bkv[:, 1, :].reshape(1, D),
        "bp": get("L0_xattn_bp").reshape(1, D),
        "ln_g": get("L0_ffn_ln_g").reshape(1, D),
        "ln_b": get("L0_ffn_ln_b").reshape(1, D),
        "router": get("L0_ffn_router_w"),
        "W1": get("L0_ffn_W1"),
        "W2": get("L0_ffn_W2"),
        "Wo": get("L0_ffn_Wo"),
        "par": par,
        "bo": get("L0_ffn_bo"),
        "const": constants(),
    }
    nc = bacc.Bacc("TRN2", target_bir_lowering=False, num_devices=1)
    feed, aps = {}, {}
    for name, v in arrays.items():
        v = np.ascontiguousarray(v)
        feed[f"in_{name}"] = v
        aps[name] = nc.dram_tensor(f"in_{name}", v.shape, mybir.dt.from_np(v.dtype),
                                   kind="ExternalInput").ap()
    out = nc.dram_tensor("out_rows", [ROWS, D], F32, kind="ExternalOutput").ap()
    build(nc, aps, out)
    r = run_bass_kernel_spmd(nc, [feed], core_ids=[0])
    return r.results[0]["out_rows"][0:TOKENS].reshape(BATCH, SEQ, D)
```

```python
from contextlib import ExitStack

import numpy as np

import concourse.bass as bass
from concourse import mybir
from concourse.alu_op_type import AluOpType as ALU

F32 = mybir.dt.float32
F32R = mybir.dt.float32r
BF16 = mybir.dt.bfloat16
I32 = mybir.dt.int32
U32 = mybir.dt.uint32
ACTF = mybir.ActivationFunctionType
AXX = mybir.AxisListType.X

P = 128
BATCH, SEQ, D = 16, 256, 256
CTX = 77
HEADS, HD = 16, 16
EXPERTS, HIDDEN = 8, 1024
EPS = 1e-5
CLIP_OUT = 10000.0
CLIP_GATE = 20.0

TOKENS = BATCH * SEQ
NT = TOKENS // P
DC = D // P
HC = HIDDEN // P
HPC = HEADS // DC
HPB = HPC // 2
HALF = HPB * HD
KEYS = HEADS * CTX
KB = -(-KEYS // P)
TAIL = KEYS - (KB - 1) * P
BLOCK_HEADS = 3
VW = HD + 1

TILE = 512
SUBS = TILE // P
MIN_TILES = -(-2 * TOKENS // TILE)
MAX_TILES = (2 * TOKENS + EXPERTS * (TILE - 1)) // TILE
SLOT_BLOCKS = MAX_TILES * SUBS
ROWS = TOKENS + TILE

C_IDENT = 0
C_TRI = C_IDENT + P
C_IOTA = C_TRI + P
C_KMASK = C_IOTA + P
C_VMASK = C_KMASK + HPB
C_TOKEN = C_VMASK + KB * BLOCK_HEADS
C_DUMP = C_TOKEN + NT
C_THR = C_DUMP + SLOT_BLOCKS
NTHR = -(-TOKENS // TILE)
C_END = C_THR + NTHR

X_G, X_B, X_B1, X_B2 = 0, DC, 2 * DC, 2 * DC + HC
X_END = 2 * DC + 2 * HC


def block_heads(i):
    first = i * P // CTX
    last = min(i * P + P - 1, KEYS - 1) // CTX
    return first, last - first + 1


def constants():
    c = np.zeros((P, C_END), np.float32)
    p = np.arange(P)
    c[:, C_IDENT:C_IDENT + P] = np.eye(P)
    c[:, C_TRI:C_TRI + P] = p[:, None] < p[None, :]
    c[:, C_IOTA:C_IOTA + P] = p[None, :]
    c[:, C_KMASK:C_KMASK + HPB] = (p[:, None] // HD) % HPB == np.arange(HPB)[None, :]
    for i in range(KB):
        first, n = block_heads(i)
        for j in range(BLOCK_HEADS):
            c[:, C_VMASK + i * BLOCK_HEADS + j] = (i * P + p) // CTX == first + j
    c[:, C_TOKEN:C_TOKEN + NT] = 1 + p[:, None] + P * np.arange(NT)[None, :]
    c[:, C_DUMP:C_DUMP + SLOT_BLOCKS] = (TOKENS + 1 + p[:, None]
                                         + P * (np.arange(SLOT_BLOCKS)[None, :] % SUBS))
    c[:, C_THR:C_THR + NTHR] = TILE * np.arange(NTHR)[None, :]
    return c


class Queue:

    def __init__(self, sem):
        self.sem, self.count, self.items, self.reached = sem, 0, [], {}

    def do(self, fn):
        self.items.append(fn)

    def sig(self, fn):
        self.count += 1
        self.items.append(lambda e: fn(e).then_inc(self.sem, 1))
        return self.sem, self.count

    def wait(self, *tokens):
        for sem, value in tokens:
            if self.reached.get(id(sem), 0) < value:
                self.reached[id(sem)] = value
                self.items.append(lambda e, sem=sem, value=value: e.wait_ge(sem, value))

    def then(self, fn):
        token = self.sig(fn)
        self.wait(token)
        return token

    def dma(self, flow, out, in_):
        flow.count += 16
        self.items.append(lambda e: e.dma_start(out, in_).then_inc(flow.sem, 16))
        return flow.sem, flow.count

    def count_tiles(self, tiles):
        self.tiles = tiles

    def emit(self, engine, start=0):
        for i in range(start, len(self.items)):
            item = self.items[i]
            if isinstance(item, Fork):
                with engine.If(self.tiles > item.tile):
                    self.emit(engine, i + 1)
                with engine.Else():
                    for last in item.ending:
                        last(engine)
                return
            item(engine)


class Fork:

    def __init__(self, tile, ending):
        self.tile, self.ending = tile, ending


class Flow:

    def __init__(self, sem):
        self.sem, self.count = sem, 0

    @property
    def token(self):
        return self.sem, self.count


def build(nc, a, out):
    ctx = ExitStack()

    scope = [ctx]

    def sb(name, shape, dt=F32):
        return scope[-1].enter_context(nc.sbuf_tensor(name, shape, dt))

    def sem(name):
        return ctx.enter_context(nc.semaphore(name))

    def flow(name):
        return Flow(sem(name))

    PR = 4
    with ctx:
        z_rows = nc.dram_tensor("z_rows", [ROWS, D], F32, kind="Internal").ap()
        v_flat = nc.dram_tensor("v_flat", [BATCH, KEYS, VW], F32, kind="Internal").ap()

        pe, act, dve, pool, sp = (Queue(sem(n)) for n in
                                  ("pe_done", "act_done", "dve_done", "pool_done", "sp_done"))
        f_const, f_rows = flow("f_const"), flow("f_rows")
        f_kv, f_wq, f_wp = flow("f_kv"), flow("f_wq"), flow("f_wp")
        f_x = [flow(f"f_x{i}") for i in range(8)]
        f_ctx = [flow(f"f_ctx{i}") for i in range(2)]
        f_vstore = [flow(f"f_vstore{i}") for i in range(2)]
        f_vload = [flow(f"f_vload{i}") for i in range(2)]
        f_x1 = [flow(f"f_x1_{i}") for i in range(3)]
        f_z = [flow(f"f_z{i}") for i in range(3)]
        f_dump = flow("f_dump")
        f_raw = [flow(f"f_raw{i}") for i in range(3)]
        f_par = [flow(f"f_par{i}") for i in range(PR)]
        f_gather = [flow(f"f_gather{i}") for i in range(2)]
        f_scatter = flow("f_scatter")

        banks = [ctx.enter_context(nc.psum_tensor(f"bank{i}", [P, 512], F32)) for i in range(8)]

        const = sb("const", [P, C_END])
        ident = const[:, C_IDENT:C_IDENT + P]
        half = sb("half", [P, 1])
        zeros = sb("zeros", [P, D])
        logits = sb("logits", [P, NT, EXPERTS])
        best = sb("best", [P, NT, 8])
        best_idx = sb("best_idx", [P, NT, 8], U32)
        tri = sb("tri", [P, P], BF16)
        ones = sb("ones", [P, P], BF16)
        no_sums = sb("no_sums", [P, NT + 1])
        scope.append(ExitStack())
        wq, wk, wv, wp = (sb(n, [P, DC, D]) for n in ("wq", "wk", "wv", "wp"))
        router = sb("router", [P, DC, EXPERTS])
        qk_bias = sb("qk_bias", [P, 2 * DC])
        rows = sb("rows", [P, 4, D])
        bv_row, bp_row, g_row, b_row = (rows[:, i, :] for i in range(4))

        sp.dma(f_const, const[:, :], a["const"])
        sp.dma(f_const, qk_bias[:, :], a["qk_bias"])
        t_const = f_const.token


        XR, XBR, XFR = 8, 8, 4
        xs = [sb(f"xs{i}", [P, D]) for i in range(XR)]
        cs = [sb(f"cs{i}", [CTX, D]) for i in range(2)]
        c_t = sb("c_t", [P, DC, CTX])
        k_t = sb("k_t", [P, DC, CTX])
        k_h = sb("k_h", [P, DC, CTX], F32R)
        k_l = sb("k_l", [P, DC, CTX])
        k_blocks = [sb(f"k_blocks{i}", [P, 2, DC, HPB, CTX], F32R) for i in range(2)]
        v_sb = [sb(f"v_sb{i}", [CTX, HEADS, VW]) for i in range(2)]
        v_rep = [sb(f"v_rep{i}", [P, KB, VW]) for i in range(2)]
        v_blocks = [sb(f"v_blocks{i}", [P, KB, BLOCK_HEADS, VW]) for i in range(2)]
        xn = [sb(f"xn{i}", [P, D]) for i in range(2)]
        xn_t = [sb(f"xn_t{i}", [P, DC, SEQ]) for i in range(2)]
        q_t = sb("q_t", [P, DC, SEQ])
        q_h = [sb(f"q_h{i}", [P, DC, SEQ], F32R) for i in range(2)]
        q_l = [sb(f"q_l{i}", [P, DC, SEQ], F32R) for i in range(2)]
        probs = [sb(f"probs{i}", [P, HEADS, CTX]) for i in range(2)]
        probs_t = [sb(f"probs_t{i}", [P, KB, P]) for i in range(2)]
        attn = [sb(f"attn{i}", [P, D]) for i in range(2)]
        attn_t = [sb(f"attn_t{i}", [P, DC, P]) for i in range(2)]
        xb = [sb(f"xb{i}", [P, D]) for i in range(XBR)]
        x1 = [sb(f"x1_{i}", [P, D]) for i in range(3)]
        y = [sb(f"y{i}", [P, D]) for i in range(2)]
        xf = [sb(f"xf{i}", [P, D]) for i in range(XFR)]
        xf_t = [sb(f"xf_t{i}", [P, DC, P]) for i in range(2)]
        z = [sb(f"z{i}", [P, D]) for i in range(3)]
        small = sb("small", [P, NT, 16])
        maxes = [sb(f"maxes{i}", [P, HEADS]) for i in range(2)]
        recip = [sb(f"recip{i}", [P, HEADS]) for i in range(2)]
        stats = sb("stats", [P, 3, NT, 6])

        score_bank = banks[0:3]
        trans_bank = banks[3:5]
        value_bank = banks[5]
        misc_bank = banks[6:8]
        score_free = [None] * 3
        trans_free = [None] * 2
        value_free = None
        misc_free = [None, None]
        turn = {"misc": 0, "score": 0, "trans": 0}

        def take(kind, free, queue):
            n = turn[kind] % len(free)
            turn[kind] += 1
            if free[n]:
                queue.wait(free[n])
            return n

        t = {}

        SCALE = 1.0 / float(np.sqrt(HD))
        bq_scaled = sb("bq_scaled", [P, DC])
        dve.wait(t_const)
        t_bq = dve.sig(lambda e: e.tensor_scalar(bq_scaled[:, :], qk_bias[:, 0:DC], SCALE, None,
                                                 ALU.mult))
        dve.sig(lambda e: e.tensor_copy(tri[:, :], const[:, C_TRI:C_TRI + P]))
        dve.sig(lambda e: e.memset(ones[:, :], 1.0))
        dve.sig(lambda e: e.memset(no_sums[:, :], 0.0))
        t_half = pool.sig(lambda e: e.memset(half[:, :], -0.5))
        t_zero = pool.sig(lambda e: e.memset(zeros[:, :], 0.0))
        t_ones = [pool.sig(lambda e, i=i: e.memset(v_sb[i][:, :, HD:VW], 1.0)) for i in range(2)]

        def load_x(i):
            if i >= XR:
                sp.wait(t["xb", i - XR], t["xn", i - XR])
            t["x", i] = sp.dma(f_x[i % XR], xs[i % XR][:, :], a["x"][i * P:(i + 1) * P, :])

        def load_ctx(b):
            if b >= 2:
                sp.wait(t["ctx_t", b - 2])
            t["ctx", b] = sp.dma(f_ctx[b % 2], cs[b % 2][:, :], a["ctx"][b * CTX:(b + 1) * CTX, :])

        def rsqrt_on_pool(dst, src):
            pool.then(lambda e: e.tensor_scalar(dst, src, EPS, None, ALU.add))
            return pool.then(lambda e: e.tensor_tensor(dst, dst, half[:, :], ALU.pow))

        def sum_rows(which, i, src):
            t["sums", which, i] = dve.sig(lambda e: e.bn_stats(stats[:, which, i, :], src))

        def mean_variance(which, i):
            dve.wait(t["sums", which, i])
            return dve.sig(lambda e: e.bn_aggr(small[:, i, 4 * which:4 * which + 2],
                                               stats[:, which, i, :]))

        def transpose_ctx(b):
            n = take("misc", misc_free, pe)
            pe.wait(t["ctx", b], t_const)
            ps = misc_bank[n]
            for c in range(DC):
                tok = pe.sig(lambda e, c=c: e.transpose(ps[:, c * CTX:(c + 1) * CTX],
                                                        cs[b % 2][:, c * P:(c + 1) * P],
                                                        ident[0:CTX, 0:CTX]))
            t["ctx_t", b] = tok
            act.wait(tok)
            if b:
                act.wait(t["kv_mm", b - 1])
            tok = act.sig(lambda e: e.activation(c_t[:, :, :], ps[:, 0:DC * CTX].rearrange(
                "p (c k) -> p c k", c=DC), ACTF.Copy))
            misc_free[n] = tok
            t["c_t", b] = tok

        def keys_values(b):
            n = take("misc", misc_free, pe)
            pe.wait(t["c_t", b], t_kv)
            psk = misc_bank[n]
            for m in range(DC):
                for c in range(DC):
                    tk = pe.sig(lambda e, m=m, c=c: e.matmul(
                        psk[:, m * CTX:(m + 1) * CTX], wk[:, c, m * P:(m + 1) * P], c_t[:, c, :],
                        start=(c == 0), stop=(c == DC - 1)))
            nv = take("misc", misc_free, pe)
            psv = misc_bank[nv]
            for c in range(DC):
                tv = pe.sig(lambda e, c=c: e.matmul(psv[0:CTX, 0:D], c_t[:, c, :], wv[:, c, :],
                                                    start=(c == 0), stop=(c == DC - 1)))
            t["kv_mm", b] = tv
            act.wait(tk, t_const)
            if b:
                act.wait(t["k_l", b - 1], t["high_blocks", b - 1])
            for m in range(DC):
                tok = act.sig(lambda e, m=m: e.activation(
                    k_t[:, m, :], psk[:, m * CTX:(m + 1) * CTX], ACTF.Identity,
                    bias=qk_bias[:, DC + m:DC + m + 1]))
            misc_free[n] = tok
            act.wait(tok)
            t_high = act.sig(lambda e: e.activation(k_h[:, :, :], k_t[:, :, :], ACTF.Copy))
            t["k_h", b] = t_high
            t["v_mm", b] = tv, nv

        def add_value_bias(b):
            tv, nv = t["v_mm", b]
            psv = misc_bank[nv]
            dve.wait(tv, t_rows_in, t_ones[1])
            if b >= 2:
                dve.wait(t["v_store", b - 2])
            tok = dve.sig(lambda e: e.tensor_tensor(
                v_sb[b % 2][:, :, 0:HD],
                psv[0:CTX, 0:D].rearrange("k (h d) -> k h d", h=HEADS),
                bv_row[0:CTX, :].rearrange("k (h d) -> k h d", h=HEADS), ALU.add))
            misc_free[nv] = tok
            sp.wait(tok)
            t["v_store", b] = sp.dma(f_vstore[b % 2],
                                     v_flat[b].rearrange("(h k) d -> k h d", h=HEADS),
                                     v_sb[b % 2][:, :, :])

        def spread_high_keys(b):
            act.wait(t["k_h", b])
            if b >= 2:
                act.wait(t["scores", 2 * (b - 2) + 1])
            for h in range(HPB):
                t["high_blocks", b] = act.sig(lambda e, h=h: e.activation(
                    k_blocks[b % 2][:, 0, :, h, :], k_h[:, :, :].bitcast(F32), ACTF.Copy,
                    scale=const[:, C_KMASK + h:C_KMASK + h + 1]))

        def low_keys(b):
            dve.wait(t["k_h", b])
            if b:
                dve.wait(t["low_blocks", b - 1])
            t["k_l", b] = dve.sig(lambda e: e.tensor_tensor(
                k_l[:, :, :], k_t[:, :, :], k_h[:, :, :].bitcast(F32), ALU.subtract))

        def spread_low_keys(b):
            pool.wait(t["k_l", b])
            if b >= 2:
                pool.wait(t["scores", 2 * (b - 2) + 1])
            for m in range(DC):
                t["low_blocks", b] = pool.sig(lambda e, m=m: e.tensor_tensor(
                    k_blocks[b % 2][:, 1, m, :, :],
                    k_l[:, m, :].unsqueeze(1).broadcast_to([P, HPB, CTX]),
                    const[:, C_KMASK:C_KMASK + HPB].unsqueeze(2).broadcast_to([P, HPB, CTX]),
                    ALU.mult))

        def load_values(b):
            sp.wait(t["v_store", b])
            if b >= 2:
                sp.wait(t["v_blocks", b - 2])
            full = (KB - 1) * P
            sp.dma(f_vload[b % 2], v_rep[b % 2][:, 0:KB - 1, :],
                   v_flat[b][0:full, :].rearrange("(i p) d -> p i d", p=P))
            t["v_load", b] = sp.dma(f_vload[b % 2], v_rep[b % 2][0:TAIL, KB - 1, :],
                                    v_flat[b][full:KEYS, :])

        def spread_values(b):
            pool.wait(t["v_load", b], t_const)
            if b >= 2:
                pool.wait(t["values", 2 * (b - 2) + 1])
            vm = const[:, C_VMASK:C_VMASK + KB * BLOCK_HEADS].rearrange(
                "p (i j) -> p i j", i=KB)
            for j in range(BLOCK_HEADS):
                for parts, lo, hi in ((P, 0, KB - 1), (TAIL, KB - 1, KB)):
                    tok = pool.sig(lambda e, j=j, parts=parts, lo=lo, hi=hi: e.tensor_tensor(
                        v_blocks[b % 2][0:parts, lo:hi, j, :], v_rep[b % 2][0:parts, lo:hi, :],
                        vm[0:parts, lo:hi, j:j + 1].broadcast_to([parts, hi - lo, VW]),
                        ALU.mult))
            t["v_blocks", b] = tok

        def x_sums(i):
            dve.wait(t["x", i])
            sum_rows(0, i, xs[i % XR][:, :])

        def x_stats(i):
            tok = mean_variance(0, i)
            pool.wait(tok, t_half)
            sm = small[:, i, :]
            t["x_stats", i] = rsqrt_on_pool(sm[:, 2:3], sm[:, 1:2])

        def x_norm(i):
            src, sm = xs[i % XR], small[:, i, :]
            dve.wait(t["x_stats", i])
            if i >= 2:
                dve.wait(t["xn_t", i - 2])
            t["xn", i] = dve.sig(lambda e: e.tensor_scalar(
                xn[i % 2][:, :], src[:, :], sm[:, 0:1], sm[:, 2:3], ALU.subtract, ALU.mult))
            pool.wait(t_rows_in)
            if i >= XBR:
                pool.wait(t["x1", i - XBR])
            t["xb", i] = pool.sig(lambda e: e.tensor_tensor(
                xb[i % XBR][:, :], src[:, :], bp_row, ALU.add))

        def transpose_xn(i):
            b, s = divmod(i, 2)
            n = take("misc", misc_free, pe)
            ps = misc_bank[n]
            pe.wait(t["xn", i], t_const)
            for c in range(DC):
                tok = pe.sig(lambda e, c=c: e.transpose(
                    ps[:, c * P:(c + 1) * P], xn[i % 2][:, c * P:(c + 1) * P], ident))
            t["xn_t", i] = tok
            act.wait(tok)
            if b >= 2:
                act.wait(t["q_mm", b - 2])
            tok = act.sig(lambda e: e.activation(
                xn_t[b % 2][:, :, s * P:(s + 1) * P],
                ps[:, 0:DC * P].rearrange("p (c k) -> p c k", c=DC), ACTF.Copy))
            misc_free[n] = tok
            t["xn_t_sb", i] = tok

        def queries(b):
            n = take("misc", misc_free, pe)
            ps = misc_bank[n]
            pe.wait(t["xn_t_sb", 2 * b + 1], t_wq)
            for m in range(DC):
                for c in range(DC):
                    tok = pe.sig(lambda e, m=m, c=c: e.matmul(
                        ps[:, m * SEQ:(m + 1) * SEQ], wq[:, c, m * P:(m + 1) * P],
                        xn_t[b % 2][:, c, :], start=(c == 0), stop=(c == DC - 1)))
            t["q_mm", b] = tok
            act.wait(tok, t_bq)
            if b:
                act.wait(t["q", b - 1])
            for m in range(DC):
                tok = act.sig(lambda e, m=m: e.activation(
                    q_t[:, m, :], ps[:, m * SEQ:(m + 1) * SEQ], ACTF.Identity,
                    bias=bq_scaled[:, m:m + 1], scale=SCALE))
            misc_free[n] = tok
            act.wait(tok)
            if b >= 2:
                act.wait(t["scores", 2 * (b - 2) + 1])
            tok = act.sig(lambda e: e.activation(q_h[b % 2][:, :, :], q_t[:, :, :], ACTF.Copy))
            t["q_h", b] = tok

        def low_queries(b):
            dve.wait(t["q_h", b])
            t["q", b] = dve.sig(lambda e: e.tensor_tensor(
                q_l[b % 2][:, :, :], q_t[:, :, :], q_h[b % 2][:, :, :].bitcast(F32),
                ALU.subtract))

        def scores(i, m):
            b, s = divmod(i, 2)
            pe.wait(t["q", b], t["high_blocks", b], t["low_blocks", b])
            ready = []
            for g in range(2):
                n = take("score", score_free, pe)
                for k, (qs, w) in enumerate(((q_h, 0), (q_l, 0), (q_h, 1))):
                    tok = pe.sig(lambda e, n=n, g=g, qs=qs, w=w, k=k: e.matmul(
                        score_bank[n][:, 0:HPB * CTX],
                        qs[b % 2][g * HALF:(g + 1) * HALF, m, s * P:(s + 1) * P],
                        k_blocks[b % 2][g * HALF:(g + 1) * HALF, w, m, :, :].rearrange(
                            "p h k -> p (h k)"), start=(k == 0), stop=(k == 2)))
                ready.append((n, tok))
            t["scores", i] = tok
            if m == 0 and i >= 2:
                dve.wait(t["probs_t", i - 2])
            views = [score_bank[n][:, 0:HPB * CTX].rearrange("p (h k) -> p h k", h=HPB)
                     for n, _ in ready]
            heads = [slice(m * HPC + g * HPB, m * HPC + (g + 1) * HPB) for g in range(2)]
            found = []
            for (n, tok), view, hs in zip(ready, views, heads):
                dve.wait(tok)
                found.append(dve.sig(lambda e, view=view, hs=hs: e.tensor_reduce(
                    maxes[i % 2][:, hs], view, AXX, ALU.max)))
            for (n, _), view, hs, tok in zip(ready, views, heads, found):
                dve.wait(tok)
                tok = dve.sig(lambda e, view=view, hs=hs: e.tensor_tensor(
                    probs[i % 2][:, hs, :], view,
                    maxes[i % 2][:, hs].unsqueeze(2).broadcast_to([P, HPB, CTX]),
                    ALU.subtract))
                score_free[n] = tok
            t["less_max", i, m] = tok

        def exp_scores(i, m):
            act.wait(t["less_max", i, m])
            part = probs[i % 2][:, m * HPC:(m + 1) * HPC, :]
            t["probs", i, m] = act.sig(lambda e: e.activation(part, part, ACTF.Exp))

        def transpose_probs(i, g):
            n = take("trans", trans_free, pe)
            ps = trans_bank[n]
            flat = probs[i % 2][:, :, :].rearrange("p h k -> p (h k)")
            blocks = list(range(4 * g, min(4 * g + 4, KB)))
            pe.wait(t["probs", i, 0 if (blocks[-1] + 1) * P <= HPC * CTX else 1])
            for j, k in enumerate(blocks):
                size = P if k < KB - 1 else TAIL
                tok = pe.sig(lambda e, j=j, k=k, size=size: e.transpose(
                    ps[0:size, j * P:(j + 1) * P], flat[:, k * P:k * P + size], ident))
            t["probs_t", i] = tok
            act.wait(tok)
            if i >= 2:
                act.wait(t["values", i - 2])
            whole = [k for k in blocks if k < KB - 1]
            pieces = [(P, 0, len(whole))] + ([(TAIL, len(whole), len(blocks))]
                                             if len(whole) < len(blocks) else [])
            for parts, lo, hi in pieces:
                dst = probs_t[i % 2][0:parts, blocks[0] + lo:blocks[0] + hi, :]
                src = ps[0:parts, lo * P:hi * P].rearrange("p (j k) -> p j k", k=P)
                tok = act.sig(lambda e, dst=dst, src=src: e.activation(dst, src, ACTF.Copy))
            trans_free[n] = tok
            t["probs_t_sb", i, g] = tok

        def values(i):
            b = i // 2
            if value_free:
                pe.wait(value_free)
            pe.wait(t["v_blocks", b])
            for k in range(KB):
                if k % 4 == 0:
                    pe.wait(t["probs_t_sb", i, k // 4])
                first, nh = block_heads(k)
                size = P if k < KB - 1 else TAIL
                tok = pe.sig(lambda e, k=k, first=first, nh=nh, size=size: e.matmul(
                    value_bank[:, first * VW:(first + nh) * VW],
                    probs_t[i % 2][0:size, k, :],
                    v_blocks[b % 2][0:size, k, 0:nh, :].rearrange("p j d -> p (j d)"),
                    start=(k == 0), stop=(k == KB - 1), skip_group_check=True))
            t["values", i] = tok
            dve.wait(tok)
            view = value_bank[:, 0:HEADS * VW].rearrange("p (h d) -> p h d", h=HEADS)
            t["recip", i] = dve.sig(lambda e: e.reciprocal(recip[i % 2][:, :].unsqueeze(2),
                                                           view[:, :, HD:VW]))

        def divide(i):
            nonlocal value_free
            view = value_bank[:, 0:HEADS * VW].rearrange("p (h d) -> p h d", h=HEADS)
            dve.wait(t["recip", i])
            if i >= 2:
                dve.wait(t["attn_t", i - 2])
            tok = dve.sig(lambda e: e.tensor_tensor(
                attn[i % 2][:, :].rearrange("p (h d) -> p h d", h=HEADS), view[:, :, 0:HD],
                recip[i % 2][:, :].unsqueeze(2).broadcast_to([P, HEADS, HD]), ALU.mult))
            value_free = tok
            t["attn", i] = tok

        def transposed_tile(i, src, src_token, dst, dst_readers, name):
            n = take("misc", misc_free, pe)
            ps = misc_bank[n]
            pe.wait(src_token)
            for c in range(DC):
                tok = pe.sig(lambda e, c=c: e.transpose(
                    ps[:, c * P:(c + 1) * P], src[:, c * P:(c + 1) * P], ident))
            t[name, i] = tok
            act.wait(tok, *dst_readers)
            tok = act.sig(lambda e: e.activation(
                dst[:, :, :], ps[:, 0:DC * P].rearrange("p (c k) -> p c k", c=DC), ACTF.Copy))
            misc_free[n] = tok
            return tok

        def transpose_attn(i):
            t["attn_t_sb", i] = transposed_tile(
                i, attn[i % 2], t["attn", i], attn_t[i % 2],
                [t["proj", i - 2]] if i >= 2 else [], "attn_t")

        def project(i):
            n = take("misc", misc_free, pe)
            ps = misc_bank[n]
            pe.wait(t["attn_t_sb", i], t_wp)
            for c in range(DC):
                tok = pe.sig(lambda e, c=c: e.matmul(ps[:, 0:D], attn_t[i % 2][:, c, :],
                                                     wp[:, c, :], start=(c == 0),
                                                     stop=(c == DC - 1)))
            t["proj", i] = tok
            dve.wait(tok, t["xb", i])
            if i >= 3:
                dve.wait(t["x1_store", i - 3])
            tok = dve.sig(lambda e: e.tensor_tensor(x1[i % 3][:, :], ps[:, 0:D], xb[i % XBR][:, :],
                                                    ALU.add))
            misc_free[n] = tok
            t["x1", i] = tok
            sp.wait(tok)
            t["x1_store", i] = sp.dma(f_x1[i % 3], out[i * P:(i + 1) * P, :], x1[i % 3][:, :])

        def x1_sums(i):
            dve.wait(t["x1", i])
            sum_rows(1, i, x1[i % 3][:, :])

        def x1_stats(i):
            tok = mean_variance(1, i)
            pool.wait(tok)
            sm = small[:, i, :]
            r1, r2 = sm[:, 12:13], sm[:, 13:14]
            rsqrt_on_pool(r1, sm[:, 5:6])
            pool.then(lambda e: e.tensor_tensor(r2, r1, r1, ALU.mult))
            pool.then(lambda e: e.tensor_tensor(r2, r2, sm[:, 5:6], ALU.mult))
            rsqrt_on_pool(r2, r2)
            t["x1_stats", i] = pool.sig(lambda e: e.tensor_tensor(sm[:, 6:7], r1, r2, ALU.mult))

        def x1_norm(i):
            sm = small[:, i, :]
            dve.wait(t["x1_stats", i])
            if i >= 2:
                dve.wait(t["xf", i - 2])
            tok = dve.sig(lambda e: e.tensor_scalar(y[i % 2][:, :], x1[i % 3][:, :], sm[:, 4:5],
                                                    sm[:, 6:7], ALU.subtract, ALU.mult))
            pool.wait(tok)
            if i >= XFR:
                pool.wait(t["xf_t", i - XFR], t["z", i - XFR])
            pool.then(lambda e: e.tensor_tensor(xf[i % XFR][:, :], y[i % 2][:, :], g_row,
                                                ALU.mult))
            t["xf", i] = pool.sig(lambda e: e.tensor_tensor(xf[i % XFR][:, :],
                                                            xf[i % XFR][:, :], b_row, ALU.add))

        def xf_sums(i):
            dve.wait(t["xf", i])
            sum_rows(2, i, xf[i % XFR][:, :])

        def xf_stats(i):
            tok = mean_variance(2, i)
            sm = small[:, i, :]
            pool.wait(tok)
            t["xf_stats", i] = rsqrt_on_pool(sm[:, 10:11], sm[:, 9:10])

        def finish_norm(i):
            sm = small[:, i, :]
            dve.wait(t["xf_stats", i])
            if i >= 3:
                dve.wait(t["z_store", i - 3])
            tok = dve.sig(lambda e: e.tensor_scalar(z[i % 3][:, :], xf[i % XFR][:, :], sm[:, 8:9],
                                                    sm[:, 10:11], ALU.subtract, ALU.mult))
            t["z", i] = tok
            sp.wait(tok)
            t["z_store", i] = sp.dma(f_z[i % 3], z_rows[i * P:(i + 1) * P, :], z[i % 3][:, :])

        def transpose_xf(i):
            t["xf_t_sb", i] = transposed_tile(
                i, xf[i % XFR], t["xf", i], xf_t[i % 2],
                [t["logits_mm", i - 2]] if i >= 2 else [], "xf_t")

        def route_logits(i):
            n = take("misc", misc_free, pe)
            ps = misc_bank[n]
            pe.wait(t["xf_t_sb", i], t_wp)
            for c in range(DC):
                tok = pe.sig(lambda e, c=c: e.matmul(ps[:, 0:EXPERTS], xf_t[i % 2][:, c, :],
                                                     router[:, c, :], start=(c == 0),
                                                     stop=(c == DC - 1)))
            t["logits_mm", i] = tok
            act.wait(tok)
            tok = act.sig(lambda e: e.activation(logits[:, i, :], ps[:, 0:EXPERTS], ACTF.Copy))
            misc_free[n] = tok
            t["logits", i] = tok

        def best_experts(i):
            dve.wait(t["logits", i])
            t["best_logits", i] = dve.sig(lambda e: e.max(best[:, i, :], logits[:, i, :]))

        def best_numbers(i):
            dve.wait(t["best_logits", i])
            t["best", i] = dve.sig(lambda e: e.max_index(best_idx[:, i, :], best[:, i, :],
                                                         logits[:, i, :]))

        def load_weights(fl, dst, n):
            return sp.dma(fl, dst[:, :, :], a[n].rearrange("(c p) n -> p c n", p=P))

        load_x(0)
        load_x(1)
        load_ctx(0)
        load_x(2)
        load_weights(f_kv, wk, "wk")
        load_x(3)
        t_kv = load_weights(f_kv, wv, "wv")
        t_wq = load_weights(f_wq, wq, "wq")
        for i, n in enumerate(("bv", "bp", "ln_g", "ln_b")):
            t_rows_in = sp.dma(f_rows, rows[:, i, :], a[n].broadcast_to([P, D]))
        load_ctx(1)
        load_weights(f_wp, wp, "wp")
        t_wp = load_weights(f_wp, router, "router")
        for i in range(4, XR):
            load_x(i)
        sp.wait(t_zero)
        for s in range(SUBS):
            dump_rows = slice(TOKENS + s * P, TOKENS + (s + 1) * P)
            sp.dma(f_dump, z_rows[dump_rows, :], zeros[:, :])
            sp.dma(f_dump, out[dump_rows, :], zeros[:, :])

        def step(fn, tile, *more):
            if 0 <= tile < NT:
                fn(tile, *more)

        for i in range(-5, NT + 6):
            even = i % 2 == 0
            nb = i // 2 + 1
            if i + 7 >= XR:
                step(load_x, i + 7)
            batch = 0 <= nb < BATCH
            step(scores, i, 0)
            step(x1_norm, i - 3)
            step(transpose_probs, i - 1, 0)
            if batch and even:
                transpose_ctx(nb)
            if batch and not even:
                low_keys(nb)
            step(transpose_attn, i - 2)
            step(xf_sums, i - 4)
            step(transpose_probs, i - 1, 1)
            if batch and not even:
                spread_low_keys(nb)
                load_values(nb)
                spread_high_keys(nb)
                queries(nb)
            step(scores, i, 1)
            step(transpose_probs, i - 1, 2)
            step(xf_stats, i - 4)
            step(project, i - 2)
            step(transpose_xn, i + 3)
            step(finish_norm, i - 5)
            if batch and not even:
                low_queries(nb)
            step(x1_sums, i - 2)
            step(exp_scores, i, 1)
            step(x_sums, i + 5)
            step(x1_stats, i - 2)
            step(exp_scores, i, 0)
            step(x_stats, i + 5)
            step(values, i - 1)
            step(divide, i - 1)
            step(best_experts, i - 6)
            step(best_numbers, i - 6)
            step(x_norm, i + 4)
            if batch and not even:
                spread_values(nb)
            step(route_logits, i - 5)
            if batch and even:
                keys_values(nb)
                add_value_bias(nb)
            step(transpose_xf, i - 4)
            if batch and even and nb + 2 < BATCH:
                load_ctx(nb + 2)

        scope.pop().close()
        stage1_stores = [t[n, i] for n in ("x1_store", "z_store") for i in range(NT - 3, NT)]

        pick = sb("pick", [P, 2, NT])
        gates = sb("gates", [P, 2, NT])
        gate_sum = sb("gate_sum", [P, NT])
        silu_loaded = sb("silu_loaded", [P, 1])
        gate_h = sb("gate_h", [P, 2, NT], F32R)
        gate_l = sb("gate_l", [P, 2, NT])
        chosen = sb("chosen", [P, 2, NT, EXPERTS])
        both = sb("both", [P, NT, EXPERTS], BF16)
        totals = sb("totals", [P, NT + 1, EXPERTS])
        running = sb("running", [P, EXPERTS, NT + 1])
        place = sb("place", [P, NT, EXPERTS])
        over = sb("over", [P, EXPERTS, NTHR])
        n_tiles = sb("n_tiles", [P, EXPERTS])
        tile_end = sb("tile_end", [P, EXPERTS])
        tile_start = sb("tile_start", [P, EXPERTS])
        begun = sb("begun", [1, MAX_TILES, EXPERTS])
        tile_expert_f = sb("tile_expert_f", [1, MAX_TILES])
        tile_expert = sb("tile_expert", [1, MAX_TILES], I32)
        tile_count = sb("tile_count", [1, 1], I32)
        slot = sb("slot", [P, 2, NT])
        slot_i = sb("slot_i", [P, 2, NT], I32)
        hi_lo_i = sb("hi_lo_i", [P, 2, 2, NT], I32)
        hi_lo = sb("hi_lo", [P, 2, 2, NT])
        filled = sb("filled", [P, 2, SLOT_BLOCKS])
        dump = sb("dump", [P, SLOT_BLOCKS])
        row_of = sb("row_of", [P, SLOT_BLOCKS], I32)

        iota = const[:, C_IOTA:C_IOTA + P]
        dve.wait(t["best", NT - 1])
        tok2 = dve.then(lambda e: e.tensor_tensor(gates[:, 1, :], best[:, :, 1], best[:, :, 0],
                                                  ALU.subtract))
        act.wait(tok2)
        tok2 = act.sig(lambda e: e.activation(gates[:, 1, :], gates[:, 1, :], ACTF.Exp))
        act.sig(lambda e: e.activation(silu_loaded[:, :], half[:, :], ACTF.Silu))
        dve.then(lambda e: e.tensor_copy(pick[:, :, :], best_idx[:, :, 0:2].rearrange(
            "p t k -> p k t")))
        for k in range(2):
            tok = dve.sig(lambda e, k=k: e.tensor_tensor(
                chosen[:, k, :, :], pick[:, k, :].unsqueeze(2).broadcast_to([P, NT, EXPERTS]),
                iota[:, 0:EXPERTS].unsqueeze(1).broadcast_to([P, NT, EXPERTS]), ALU.is_equal))
        dve.wait(tok)
        tok = dve.sig(lambda e: e.tensor_tensor(both[:, :, :], chosen[:, 0, :, :],
                                                chosen[:, 1, :, :], ALU.add))
        pe.wait(tok)
        pe.wait(*[f for f in score_free if f])
        flat_both = both[:, :, :].rearrange("p t e -> p (t e)")
        nte = NT * EXPERTS
        tok_pre = pe.sig(lambda e: e.matmul(banks[0][:, 0:nte], tri[:, :], flat_both, start=True,
                                            stop=True))
        tok_tot = pe.sig(lambda e: e.matmul(banks[1][:, 0:nte], ones[:, :], flat_both, start=True,
                                            stop=True))
        dve.wait(tok2)
        dve.then(lambda e: e.tensor_scalar(gate_sum[:, :], gates[:, 1, :], 1.0, None, ALU.add))
        dve.then(lambda e: e.reciprocal(gates[:, 0, :], gate_sum[:, :]))
        tok2 = dve.sig(lambda e: e.tensor_tensor(gates[:, 1, :], gates[:, 1, :],
                                                 gates[:, 0, :], ALU.mult))
        act.wait(tok2)
        t_gate_h = act.sig(lambda e: e.activation(gate_h[:, :, :], gates[:, :, :], ACTF.Copy))
        dve.wait(tok_tot)
        dve.sig(lambda e: e.memset(totals[:, 0:1, :], 0.0))
        dve.then(lambda e: e.tensor_copy(totals[:, 1:NT + 1, :], banks[1][:, 0:nte].rearrange(
            "p (t e) -> p t e", t=NT)))
        for x in range(EXPERTS):
            tok = dve.sig(lambda e, x=x: e.tensor_tensor_scan(
                running[:, x, :], totals[:, :, x], no_sums[:, :], 0.0, ALU.add, ALU.add))
        dve.wait(tok)
        dve.then(lambda e: e.tensor_tensor(
            over[:, :, :], running[:, :, NT:NT + 1].broadcast_to([P, EXPERTS, NTHR]),
            const[:, C_THR:C_THR + NTHR].unsqueeze(1).broadcast_to([P, EXPERTS, NTHR]),
            ALU.is_gt))
        dve.then(lambda e: e.tensor_reduce(n_tiles[:, :], over[:, :, :], AXX, ALU.add))
        dve.then(lambda e: e.tensor_tensor_scan(tile_end[:, :], n_tiles[:, :],
                                                no_sums[:, 0:EXPERTS], 0.0, ALU.add, ALU.add))
        dve.then(lambda e: e.tensor_tensor(tile_start[:, :], tile_end[:, :], n_tiles[:, :],
                                           ALU.subtract))
        dve.then(lambda e: e.tensor_tensor(
            begun[:, :, :],
            tile_start[0:1, :].unsqueeze(1).broadcast_to([1, MAX_TILES, EXPERTS]),
            iota[0:1, 0:MAX_TILES].unsqueeze(2).broadcast_to([1, MAX_TILES, EXPERTS]),
            ALU.is_le))
        dve.sig(lambda e: e.tensor_copy(tile_count[:, :], tile_end[0:1, EXPERTS - 1:EXPERTS]))
        dve.then(lambda e: e.tensor_reduce(tile_expert_f[:, :], begun[:, :, :], AXX, ALU.add))
        t_tile_expert = dve.sig(lambda e: e.tensor_scalar(
            tile_expert[:, :], tile_expert_f[:, :], -1.0, None, ALU.add))
        dve.wait(t_gate_h)
        t_gates = dve.sig(lambda e: e.tensor_tensor(gate_l[:, :, :], gates[:, :, :],
                                                    gate_h[:, :, :].bitcast(F32), ALU.subtract))
        dve.wait(tok_pre)
        dve.then(lambda e: e.tensor_tensor(
            place[:, :, :], banks[0][:, 0:nte].rearrange("p (t e) -> p t e", t=NT),
            running[:, :, 0:NT].rearrange("p e t -> p t e"), ALU.add))
        dve.then(lambda e: e.scalar_tensor_tensor(
            place[:, :, :], tile_start[:, :].unsqueeze(1).broadcast_to([P, NT, EXPERTS]),
            float(TILE), place[:, :, :], ALU.mult, ALU.add))
        for k in range(2):
            dve.then(lambda e, k=k: e.tensor_tensor(chosen[:, k, :, :], chosen[:, k, :, :],
                                                    place[:, :, :], ALU.mult))
            tok = dve.sig(lambda e, k=k: e.tensor_reduce(slot[:, k, :], chosen[:, k, :, :], AXX,
                                                         ALU.add))
        dve.wait(tok)
        dve.then(lambda e: e.tensor_copy(slot_i[:, :, :], slot[:, :, :]))
        dve.sig(lambda e: e.tensor_single_scalar(hi_lo_i[:, 0, :, :], slot_i[:, :, :], 7,
                                                 ALU.logical_shift_right))
        dve.then(lambda e: e.tensor_single_scalar(hi_lo_i[:, 1, :, :], slot_i[:, :, :], P - 1,
                                                  ALU.bitwise_and))
        dve.then(lambda e: e.tensor_copy(hi_lo[:, :, :, :], hi_lo_i[:, :, :, :]))

        raw = [sb(f"raw{i}", [P, 2, HIDDEN]) for i in range(3)]
        wh = [sb(f"wh{i}", [P, 3, 2, HIDDEN], F32R) for i in range(2)]
        wl = [sb(f"wl{i}", [P, 3, 2, HIDDEN], F32R) for i in range(2)]
        par = [sb(f"par{i}", [P, X_END]) for i in range(PR)]
        bo_row = [sb(f"bo_row{i}", [P, D]) for i in range(PR)]
        FILL = 8
        scope.append(ExitStack())
        FR = 3
        at_lo = [sb(f"at_lo{i}", [P, FILL, P], F32R) for i in range(FR)]
        at_hi = [sb(f"at_hi{i}", [P, FILL, SLOT_BLOCKS]) for i in range(FR)]
        at_value = [sb(f"at_value{i}", [P, FILL, 3, SLOT_BLOCKS], F32R) for i in range(FR)]
        scope.pop().close()
        fill_bank = banks[2]

        def fill(g):
            k, i0 = divmod(g * FILL, NT)
            q = g % FR
            lo, hi = (hi_lo[:, w, k, i0:i0 + FILL] for w in (1, 0))
            if g >= FR:
                dve.wait(t["fill", g - FR])
            dve.sig(lambda e: e.tensor_tensor(
                at_lo[q][:, :, :], lo.unsqueeze(2).broadcast_to([P, FILL, P]),
                iota.unsqueeze(1).broadcast_to([P, FILL, P]), ALU.is_equal))
            shape = [P, FILL, SLOT_BLOCKS]
            tok = dve.sig(lambda e: e.tensor_tensor(
                at_hi[q][:, :, :], hi.unsqueeze(2).broadcast_to(shape),
                iota[:, 0:SLOT_BLOCKS].unsqueeze(1).broadcast_to(shape), ALU.is_equal))
            act.wait(tok)
            for n in range(FILL):
                tok_a = act.sig(lambda e, n=n: e.activation(
                    at_value[q][:, n, 0, :], at_hi[q][:, n, :], ACTF.Copy,
                    scale=const[:, C_TOKEN + i0 + n:C_TOKEN + i0 + n + 1]))
            pool.wait(tok, t_gates)
            for w, part in ((1, gate_h[:, k, i0:i0 + FILL].bitcast(F32)),
                            (2, gate_l[:, k, i0:i0 + FILL])):
                tok_p = pool.sig(lambda e, w=w, part=part: e.tensor_tensor(
                    at_value[q][:, :, w, :], at_hi[q][:, :, :],
                    part.unsqueeze(2).broadcast_to(shape), ALU.mult))
            pe.wait(tok_a, tok_p)
            for n in range(FILL):
                tok = pe.sig(lambda e, n=n: e.matmul(
                    fill_bank[:, 0:3 * SLOT_BLOCKS], at_lo[q][:, n, :],
                    at_value[q][:, n, :, :].rearrange("p w s -> p (w s)"),
                    start=(g == 0 and n == 0),
                    stop=((g + 1) * FILL == 2 * NT and n == FILL - 1)))
            t["fill", g] = tok

        zg = [sb(f"zg{i}", [P, SUBS, D]) for i in range(2)]
        xa = [sb(f"xa{i}", [P, TILE]) for i in range(DC)]
        xh = [sb(f"xh{i}", [P, DC, TILE], F32R) for i in range(2)]
        xl = [sb(f"xl{i}", [P, DC, TILE], F32R) for i in range(2)]
        gate_in = [sb(f"gate_in{i}", [P, TILE]) for i in range(3)]
        hid = [sb(f"hid{i}", [P, TILE]) for i in range(2)]
        HR = 4
        hh = [sb(f"hh{i}", [P, TILE], F32R) for i in range(HR)]
        hl = [sb(f"hl{i}", [P, TILE], F32R) for i in range(HR)]
        yo = [sb(f"yo{i}", [P, 2, D]) for i in range(2)]

        up_bank = [banks[0], banks[1]]
        gate_bank = [banks[3], banks[4]]
        down_bank = [banks[5], banks[6]]
        x_bank = [banks[2], banks[7]]

        src_of = (a["W1"].rearrange("e (c p) n -> e p c n", p=P),
                  a["W2"].rearrange("e (c p) n -> e p c n", p=P),
                  a["Wo"].rearrange("e (a m p) n -> e p a m n", a=2, p=P))
        expert_reg = {}

        def load_expert(j):
            if j == 0:
                sp.wait(t_tile_expert, *stage1_stores)
            if j >= PR:
                sp.wait(t["tile_done", j - PR])
            fl = f_par[j % PR]
            fl.count += 32

            def issue(e):
                expert_reg[j] = e.value_load(tile_expert[0:1, j:j + 1], min_val=0,
                                             max_val=EXPERTS - 1)
                e.dma_start(par[j % PR][:, :], a["par"][bass.ds(expert_reg[j], 1)].rearrange(
                    "e p n -> (e p) n")).then_inc(fl.sem, 16)
                e.dma_start(bo_row[j % PR][:, :], a["bo"][bass.ds(expert_reg[j], 1), :]
                            .broadcast_to([P, D])).then_inc(fl.sem, 16)

            sp.do(issue)
            t["par", j] = fl.token

        def load_matrix(j, w):
            if j:
                sp.wait(t["split", j - 1, w])
            fl = f_raw[w]
            fl.count += 16

            def issue(e):
                src = src_of[w][bass.ds(expert_reg[j], 1)]
                if w == 2:
                    dst = raw[w][:, :, :].rearrange("p a (m n) -> p a m n", n=D)
                    src = src.rearrange("e p a m n -> (e p) a m n")
                else:
                    dst = raw[w][:, :, :]
                    src = src.rearrange("e p c n -> (e p) c n")
                return e.dma_start(dst, src).then_inc(fl.sem, 16)

            sp.do(issue)
            t["raw", j, w] = fl.token

        def high_weights(j, w, c):
            act.wait(t["raw", j, w])
            if j >= 2:
                act.wait(t["down" if w == 2 else "up", j - 2, HC - 1])
            t["high", j, w, c] = act.sig(lambda e: e.activation(
                wh[j % 2][:, w, c, :], raw[w][:, c, :], ACTF.Copy))

        def low_weights(j, w, c):
            dve.wait(t["high", j, w, c])
            t["split", j, w] = dve.sig(lambda e: e.tensor_tensor(
                wl[j % 2][:, w, c, :], raw[w][:, c, :], wh[j % 2][:, w, c, :].bitcast(F32),
                ALU.subtract))

        def gather(j):
            if j == 0:
                pool.wait(t_rows, f_dump.token, *stage1_stores)
            if j >= 2:
                pool.wait(t["x_t", j - 2])
            fl = f_gather[j % 2]
            for s in range(SUBS):
                fl.count += 16
                blk = j * SUBS + s
                pool.do(lambda e, s=s, blk=blk: e.indirect_dma_start(
                    out=zg[j % 2][:, s, :], out_offset=None, in_=z_rows,
                    in_offset=bass.IndirectOffsetOnAxis(ap=row_of[:, blk:blk + 1], axis=0))
                    .then_inc(fl.sem, 16))
            t["gather", j] = fl.token

        def transpose_rows(j):
            pe.wait(t["gather", j])
            if j == 0:
                pe.wait(t_gate)
            for c in range(DC):
                if j:
                    pe.wait(t["xa", j - 1, c])
                for s in range(SUBS):
                    tok = pe.sig(lambda e, c=c, s=s: e.transpose(
                        x_bank[c][:, s * P:(s + 1) * P], zg[j % 2][:, s, c * P:(c + 1) * P],
                        ident))
            t["x_t", j] = tok

        def scale_rows(j, c):
            act.wait(t["x_t", j], t["par", j])
            if j:
                act.wait(t["xl", j - 1, c])
            t["xa", j, c] = act.sig(lambda e: e.activation(
                xa[c][:, :], x_bank[c][:, 0:TILE], ACTF.Identity,
                scale=par[j % PR][:, X_G + c:X_G + c + 1],
                bias=par[j % PR][:, X_B + c:X_B + c + 1]))

        def high_rows(j, c):
            act.wait(t["xa", j, c])
            if j >= 2:
                act.wait(t["up", j - 2, HC - 1])
            t["xh", j, c] = act.sig(lambda e: e.activation(xh[j % 2][:, c, :], xa[c][:, :],
                                                           ACTF.Copy))

        def low_rows(j, c):
            dve.wait(t["xh", j, c])
            t["xl", j, c] = dve.sig(lambda e: e.tensor_tensor(
                xl[j % 2][:, c, :], xa[c][:, :], xh[j % 2][:, c, :].bitcast(F32),
                ALU.subtract))

        def up(j, m):
            q, n = j % 2, (j * HC + m) % 2
            for w, ps, reader in ((1, gate_bank[n], "gate_free"), (0, up_bank[n], "gated")):
                if m == 0:
                    pe.wait(t["split", j, w])
                if (reader, j * HC + m - 2) in t:
                    pe.wait(t[reader, j * HC + m - 2])
                products = [(wh, xh[q]), (wh, xl[q]), (wl, xh[q])]
                for c in range(DC):
                    if m == 0:
                        pe.wait(t["xl", j, c])
                    for k, (ws, xx) in enumerate(products):
                        tok = pe.sig(lambda e, ws=ws, xx=xx, c=c, k=k, w=w, ps=ps: e.matmul(
                            ps[:, 0:TILE], ws[q][:, w, c, m * P:(m + 1) * P], xx[:, c, :],
                            start=(c == 0 and k == 0), stop=(c == DC - 1 and k == 2)))
                t["up" if w == 0 else "gate", j, m] = tok

        def gate_to_sbuf(j, m):
            n = j * HC + m
            gi, bias = gate_in[n % 3], par[j % PR][:, X_B2 + m:X_B2 + m + 1]
            act.wait(t["gate", j, m], t["par", j])
            if n >= 3:
                act.wait(t["gated", n - 3])
            t["gate_free", n] = act.sig(lambda e: e.activation(
                gi[:, :], gate_bank[n % 2][:, 0:TILE], ACTF.Identity, bias=bias))

        def clip_gate(j, m):
            n = j * HC + m
            gi = gate_in[n % 3]
            dve.wait(t["gate_free", n])
            t["clipped", n] = dve.sig(lambda e: e.tensor_scalar(
                gi[:, :], gi[:, :], CLIP_GATE, -CLIP_GATE, ALU.min, ALU.max))

        def silu_gate(j, m):
            n = j * HC + m
            gi = gate_in[n % 3]
            act.wait(t["clipped", n])
            t["silu", n] = act.sig(lambda e: e.activation(gi[:, :], gi[:, :], ACTF.Silu))

        def gated(j, m):
            n = j * HC + m
            gi, h, bias = gate_in[n % 3], hid[n % 2], par[j % PR][:, X_B1 + m:X_B1 + m + 1]
            dve.wait(t["silu", n], t["up", j, m])
            t["gated", n] = dve.then(lambda e: e.scalar_tensor_tensor(
                h[:, :], up_bank[n % 2][:, 0:TILE], bias, gi[:, :], ALU.add, ALU.mult))
            t["hid", n] = dve.sig(lambda e: e.tensor_scalar(
                h[:, :], h[:, :], CLIP_OUT, -CLIP_OUT, ALU.min, ALU.max))

        def high_hidden(j, m):
            n = j * HC + m
            act.wait(t["hid", n])
            if n >= HR:
                act.wait(t[("down",) + divmod(n - HR, HC)])
            t["hh", n] = act.sig(lambda e: e.activation(hh[n % HR][:, :], hid[n % 2][:, :],
                                                        ACTF.Copy))

        def low_hidden(j, m):
            n = j * HC + m
            dve.wait(t["hh", n])
            t["hidden", j, m] = dve.sig(lambda e: e.tensor_tensor(
                hl[n % HR][:, :], hid[n % 2][:, :], hh[n % HR][:, :].bitcast(F32),
                ALU.subtract))

        def down(j, m):
            q, r = j % 2, (j * HC + m) % HR
            if m == 0 and j:
                pe.wait(*[t["down_free", j - 1, s] for s in range(-(-SUBS // 2))])
            if m == 0:
                pe.wait(t["split", j, 2])
            pe.wait(t["hidden", j, m])
            for s in range(SUBS):
                ps = down_bank[s // 2]
                w_of = lambda ws: ws[q][:, 2, m // 4, (m % 4) * D:(m % 4 + 1) * D]
                for k, (hs, ws) in enumerate(((hh, wh), (hh, wl), (hl, wh))):
                    tok = pe.sig(lambda e, s=s, k=k, hs=hs, w=w_of(ws), ps=ps: e.matmul(
                        ps[:, (s % 2) * D:(s % 2 + 1) * D], hs[r][:, s * P:(s + 1) * P], w,
                        start=(m == 0 and k == 0 and s % 2 == 0),
                        stop=(m == HC - 1 and k == 2), skip_group_check=True))
            t["down", j, m] = tok

        def finish_tile(j):
            q = j % 2
            for s2 in range(-(-SUBS // 2)):
                n = min(2, SUBS - 2 * s2)
                o = yo[s2][:, 0:n, :]
                dve.wait(t["down", j, HC - 1])
                if j:
                    dve.wait(t["scattered", j - 1])
                tok = dve.then(lambda e, s2=s2, n=n, o=o: e.tensor_tensor(
                    o, down_bank[s2][:, 0:n * D].rearrange("p (s d) -> p s d", d=D),
                    bo_row[j % PR][:, :].unsqueeze(1).broadcast_to([P, n, D]), ALU.add))
                t["down_free", j, s2] = tok
                t["tile_done", j] = tok
                tok = dve.sig(lambda e, o=o: e.tensor_scalar(o, o, CLIP_OUT, -CLIP_OUT, ALU.min,
                                                             ALU.max))
                act.wait(tok, t_gate)
                for s in range(n):
                    blk = j * SUBS + 2 * s2 + s
                    tok = act.sig(lambda e, s=s, s2=s2, blk=blk: e.activation(
                        yo[s2][:, s, :], yo[s2][:, s, :], ACTF.Copy,
                        scale=filled[:, 1, blk:blk + 1]))
                    pool.wait(tok)
                    if j:
                        pool.wait(t["scattered", j - 1])
                    f_scatter.count += 16
                    pool.do(lambda e, s=s, s2=s2, blk=blk: e.indirect_dma_start(
                        out=out, out_offset=bass.IndirectOffsetOnAxis(
                            ap=row_of[:, blk:blk + 1], axis=0),
                        in_=yo[s2][:, s, :], in_offset=None, bounds_check=ROWS - 1,
                        oob_is_err=True, compute_op=ALU.add).then_inc(f_scatter.sem, 16))
            t["scattered", j] = f_scatter.token

        PIECES = {0: (1, 0), 1: (1, 1), 3: (0, 0), 4: (0, 1), 6: (2, 0), 7: (2, 1)}
        ROWS_T, ROWS_SCALE, ROWS_H, ROWS_L = 3, 4, 5, 6
        load_expert(0)
        for w in (1, 0, 2):
            load_matrix(0, w)
        first_pieces = [(w, c) for w in (1, 0) for c in range(2)]
        for q in (pe, act, dve, pool, sp):
            q.wait(t_tile_expert)
            q.do(lambda e, q=q: q.count_tiles(e.value_load(
                tile_count[0:1, 0:1], min_val=MIN_TILES, max_val=MAX_TILES)))
        groups = 2 * NT // FILL
        for g in range(groups + 2):
            if g < groups:
                fill(g)
            if 0 <= g - 1 < len(first_pieces):
                high_weights(0, *first_pieces[g - 1])
            if 0 <= g - 2 < len(first_pieces):
                low_weights(0, *first_pieces[g - 2])
        dve.wait(t["fill", 2 * NT // FILL - 1])
        dve.then(lambda e: e.tensor_copy(filled[:, :, :], fill_bank[
            :, 0:2 * SLOT_BLOCKS].rearrange("p (w s) -> p w s", w=2)))
        dve.then(lambda e: e.scalar_tensor_tensor(
            dump[:, :], filled[:, 0, :], 0.0, const[:, C_DUMP:C_DUMP + SLOT_BLOCKS],
            ALU.is_equal, ALU.mult))
        t_rows = dve.sig(lambda e: e.scalar_tensor_tensor(
            row_of[:, :], filled[:, 0, :], -1.0, dump[:, :], ALU.add, ALU.add))
        t_gate = dve.sig(lambda e: e.tensor_tensor(
            filled[:, 1, :], filled[:, 1, :], fill_bank[:, 2 * SLOT_BLOCKS:3 * SLOT_BLOCKS],
            ALU.add))
        gather(0)
        for c in range(2):
            high_weights(0, 2, c)
        for c in range(2):
            low_weights(0, 2, c)
        sp.wait(t["gather", 0])
        load_expert(1)
        for w in (1, 0, 2):
            load_matrix(1, w)
        transpose_rows(0)
        for c in range(DC):
            scale_rows(0, c)
            high_rows(0, c)
            low_rows(0, c)
        LAG = 4

        def steps(n, tiles):
            j, m = divmod(n, HC)
            in_use = j < tiles
            more = in_use and j + 1 < MAX_TILES

            def chunk(fn, n):
                if 0 <= n < tiles * HC:
                    fn(*divmod(n, HC))

            def piece(fn, n):
                j, m = divmod(n, HC)
                if n >= 0 and j + 1 < MAX_TILES and m in PIECES and in_use:
                    w, c = PIECES[m]
                    fn(j + 1, w, c)
                    if fn is low_weights and c == 1 and j + 2 < MAX_TILES:
                        load_matrix(j + 2, w)

            if m == 0 and more:
                gather(j + 1)
                if j + 2 < MAX_TILES:
                    load_expert(j + 2)
            chunk(up, n)
            chunk(high_hidden, n - 2)
            chunk(silu_gate, n - 1)
            chunk(gate_to_sbuf, n)
            if more and m == ROWS_H:
                for c in range(DC):
                    high_rows(j + 1, c)
            piece(high_weights, n)
            chunk(low_hidden, n - 2)
            chunk(gated, n - 1)
            chunk(clip_gate, n)
            if more and m == ROWS_L:
                for c in range(DC):
                    low_rows(j + 1, c)
            piece(low_weights, n - 1)
            if n >= LAG:
                jd, md = divmod(n - LAG, HC)
                down(jd, md)
                if md == HC - 1:
                    finish_tile(jd)
            if more and m == ROWS_T:
                transpose_rows(j + 1)
            if more and m == ROWS_SCALE:
                for c in range(DC):
                    scale_rows(j + 1, c)

        def end(tiles):
            for n in range(tiles * HC, tiles * HC + LAG):
                steps(n, tiles)
            pool.wait(f_scatter.token)
            sp.wait(*[f.token for f in f_raw + f_par])

        queues = (pe, act, dve, pool, sp)
        flows = f_raw + f_par + f_gather + [f_scatter]

        def fork(tiles):
            counts = [x.count for x in (*queues, *flows)]
            before = [(q.items, dict(q.reached)) for q in queues]
            tokens = dict(t)
            for q in queues:
                q.items = []
            end(tiles)
            for q, (items, reached) in zip(queues, before):
                q.items, q.reached = items + [Fork(tiles, q.items)], reached
            for x, count in zip((*queues, *flows), counts):
                x.count = count
            t.clear()
            t.update(tokens)

        for j in range(MAX_TILES):
            if j >= MIN_TILES:
                fork(j)
            for n in range(j * HC, (j + 1) * HC):
                steps(n, MAX_TILES)
        end(MAX_TILES)

        block = ctx.enter_context(nc.Block())
        block.sync(lambda e: sp.emit(e))
        block.gpsimd(lambda e: pool.emit(e))
        block.scalar(lambda e: act.emit(e))
        block.vector(lambda e: dve.emit(e))
        block.tensor(lambda e: pe.emit(e))


def kernel(**inputs):
    import concourse.bacc as bacc
    from concourse.bass_utils import run_bass_kernel_spmd

    def columns(v):
        v = np.asarray(v)
        return v.reshape(-1, P).T

    def get(name):
        return np.asarray(inputs[name])

    wkv = get("L0_xattn_Wkv").reshape(D, HEADS, 2, HD)
    bkv = get("L0_xattn_bkv").reshape(HEADS, 2, HD)
    par = np.stack([np.concatenate([columns(get(n)[e]) for n in
                                    ("L0_ffn_eg", "L0_ffn_eb", "L0_ffn_b1", "L0_ffn_b2")], axis=1)
                    for e in range(EXPERTS)])
    arrays = {
        "x": get("x").reshape(TOKENS, D),
        "ctx": get("ctx_1024").reshape(BATCH * CTX, D),
        "wq": get("L0_xattn_Wq"),
        "wk": wkv[:, :, 0, :].reshape(D, D),
        "wv": wkv[:, :, 1, :].reshape(D, D),
        "wp": get("L0_xattn_Wp"),
        "qk_bias": np.concatenate([columns(get("L0_xattn_bq")),
                                   columns(bkv[:, 0, :].reshape(D))], axis=1),
        "bv": bkv[:, 1, :].reshape(1, D),
        "bp": get("L0_xattn_bp").reshape(1, D),
        "ln_g": get("L0_ffn_ln_g").reshape(1, D),
        "ln_b": get("L0_ffn_ln_b").reshape(1, D),
        "router": get("L0_ffn_router_w"),
        "W1": get("L0_ffn_W1"),
        "W2": get("L0_ffn_W2"),
        "Wo": get("L0_ffn_Wo"),
        "par": par,
        "bo": get("L0_ffn_bo"),
        "const": constants(),
    }
    nc = bacc.Bacc("TRN2", target_bir_lowering=False, num_devices=1)
    feed, aps = {}, {}
    for name, v in arrays.items():
        v = np.ascontiguousarray(v)
        feed[f"in_{name}"] = v
        aps[name] = nc.dram_tensor(f"in_{name}", v.shape, mybir.dt.from_np(v.dtype),
                                   kind="ExternalInput").ap()
    out = nc.dram_tensor("out_rows", [ROWS, D], F32, kind="ExternalOutput").ap()
    build(nc, aps, out)
    r = run_bass_kernel_spmd(nc, [feed], core_ids=[0])
    return r.results[0]["out_rows"][0:TOKENS].reshape(BATCH, SEQ, D)
```
